# Optimizing a Trainium2 kernel written in Bass

```python
import numpy as np
import jax
import jax.numpy as jnp

def _softmax(x, axis=-1):
    return jax.nn.softmax(x, axis=axis)

def _gelu(x):
    return jax.nn.gelu(x, approximate=True)

def _silu(x):
    return jax.nn.silu(x)

def _sigmoid(x):
    return jax.nn.sigmoid(x)

def _layernorm(x, axis=-1, eps=1e-05):
    m = jnp.mean(x, axis=axis, keepdims=True)
    v = jnp.var(x, axis=axis, keepdims=True)
    return (x - m) / jnp.sqrt(v + eps)

def _scatter_add(tgt, idx, src, axis=0):
    return tgt.at[idx].add(src)

def _segment_sum(src, seg, n):
    return jax.ops.segment_sum(src, seg, n)
kernel_name = 'mk_decoder_preln_d1_seqx_r8_fc74ea'

def setup_inputs(seed: int=0):
    np.random.seed(seed)
    _w = jnp.asarray

    def _rec_inputs():
        import jax
        import jax.numpy as jnp
        _rk = jax.random.key(seed)
        x = 7.22e-05 + 1 * jax.random.normal(jax.random.fold_in(_rk, 1), (128, 64, 128), jnp.float32)
        _lenS = 64 - jax.random.randint(jax.random.fold_in(_rk, 7), (128,), 0, max(1, 64 // 4) + 1, jnp.int32)
        _lenS2 = 64 - jax.random.randint(jax.random.fold_in(_rk, 8), (128,), 0, max(1, 64 // 4) + 1, jnp.int32)
        _ctx_1024P = jax.random.normal(jax.random.fold_in(_rk, 11), (128, 16, 128), jnp.float32)
        _ctx_1024c = jax.random.dirichlet(jax.random.fold_in(_rk, 511), 0.3 * jnp.ones((16,), jnp.float32), (128, 64))
        _ctx_1024t = jnp.einsum('bsk,bkd->bsd', _ctx_1024c, _ctx_1024P)
        _ctx_1024t = _ctx_1024t * jax.lax.rsqrt(jnp.mean(jnp.square(_ctx_1024t)) + 1e-12) * 0.953939
        ctx_1024 = 4.13588e-05 + 0.999923 * (_ctx_1024t + 0.3 * jax.random.normal(jax.random.fold_in(_rk, 611), (128, 64, 128), jnp.float32))
        return (x, ctx_1024)
    x, ctx_1024 = _rec_inputs()

    def _L0_attn_setup():
        import jax, jax.numpy as jnp
        import numpy as np
        DIM = 128
        NUM_HEADS = 16
        DIM_HEAD = 64
        POOL = 8
        SCALE = DIM_HEAD ** (-0.5)
        key = jax.random.key(seed)
        k1, k2, k3, k4 = jax.random.split(key, 4)
        inner = NUM_HEADS * DIM_HEAD
        x = jax.random.normal(k1, (4, 512, DIM), dtype=jnp.float32)
        Wqkv = jax.random.normal(k2, (DIM, 3 * inner), dtype=jnp.float32) * DIM ** (-0.5)
        Wo = jax.random.normal(k3, (inner, DIM), dtype=jnp.float32) * inner ** (-0.5)
        bo = jax.random.normal(k4, (DIM,), dtype=jnp.float32) * 0.01
        return {'x': x, 'Wqkv': Wqkv, 'Wo': Wo, 'bo': bo}
    _L0_attn_all = _L0_attn_setup()
    _L0_attn_in = {k: v for k, v in _L0_attn_all.items() if k in ('Wqkv', 'Wo', 'bo')}
    del _L0_attn_all

    def _L0_xattn_setup():
        import jax, jax.numpy as jnp
        import numpy as np
        N_HEADS = 16
        D_MODEL = 128
        D_K = D_MODEL // N_HEADS
        NEG_INF = -1000000000.0

        def _split_heads(x):
            B, S, _ = x.shape
            return x.reshape(B, S, N_HEADS, D_K).transpose(0, 2, 1, 3)
        key = jax.random.key(seed)
        ks = jax.random.split(key, 7)
        B, S, D = (4, 256, D_MODEL)
        scale = 1.0 / np.sqrt(D)
        return {'query': jax.random.normal(ks[0], (B, S, D), dtype=jnp.float32), 'key': jax.random.normal(ks[1], (B, S, D), dtype=jnp.float32), 'value': jax.random.normal(ks[2], (B, S, D), dtype=jnp.float32), 'Wq': jax.random.normal(ks[3], (D, D), dtype=jnp.float32) * scale, 'Wk': jax.random.normal(ks[4], (D, D), dtype=jnp.float32) * scale, 'Wv': jax.random.normal(ks[5], (D, D), dtype=jnp.float32) * scale, 'Wo': jax.random.normal(ks[6], (D, D), dtype=jnp.float32) * scale}
    _L0_xattn_all = _L0_xattn_setup()
    _L0_xattn_in = {k: v for k, v in _L0_xattn_all.items() if k in ('Wq', 'Wk', 'Wv', 'Wo')}
    del _L0_xattn_all

    def _L0_ffn_setup():
        import jax, jax.numpy as jnp
        import numpy as np
        DIM = 128
        E = 16
        TOPK = 2
        G = 4
        TOPK_G = 2
        INTER = 64
        N_SHARED = 2
        ROUTE_SCALE = 1.0

        def _gate(xf, gate_w, gate_b):
            scores = xf @ gate_w.T
            scores = jax.nn.softmax(scores.astype(jnp.float32), axis=-1)
            orig = scores
            scores = scores + gate_b
            T = xf.shape[0]
            sg = scores.reshape(T, G, E // G)
            group_scores = jax.lax.top_k(sg, 2)[0].sum(-1)
            _, gidx = jax.lax.top_k(group_scores, TOPK_G)
            keep = jax.nn.one_hot(gidx, G).sum(axis=1) > 0
            sg = jnp.where(keep[:, :, None], sg, -jnp.inf)
            scores = sg.reshape(T, E)
            _, idx = jax.lax.top_k(scores, TOPK)
            weights = jnp.take_along_axis(orig, idx, axis=1)
            weights = (weights * ROUTE_SCALE).astype(xf.dtype)
            return (weights, idx)
        key = jax.random.key(seed)
        ks = jax.random.split(key, 16)
        s = lambda fan_in: 1.0 / np.sqrt(fan_in)
        inp = {'x': jax.random.normal(ks[0], (4, 128, DIM), dtype=jnp.float32), 'gate_w': jax.random.normal(ks[1], (E, DIM), dtype=jnp.float32) * s(DIM), 'gate_b': jnp.zeros((E,), dtype=jnp.float32), 'We1': jax.random.normal(ks[2], (E, DIM, INTER), dtype=jnp.float32) * s(DIM), 'be1': jnp.zeros((E, INTER), dtype=jnp.float32), 'We2': jax.random.normal(ks[3], (E, INTER, DIM), dtype=jnp.float32) * s(INTER), 'be2': jnp.zeros((E, DIM), dtype=jnp.float32), 'We3': jax.random.normal(ks[4], (E, DIM, INTER), dtype=jnp.float32) * s(DIM), 'be3': jnp.zeros((E, INTER), dtype=jnp.float32), 'ws1': jax.random.normal(ks[5], (DIM, N_SHARED * INTER), dtype=jnp.float32) * s(DIM), 'bs1': jnp.zeros((N_SHARED * INTER,), dtype=jnp.float32), 'ws2': jax.random.normal(ks[6], (N_SHARED * INTER, DIM), dtype=jnp.float32) * s(N_SHARED * INTER), 'bs2': jnp.zeros((DIM,), dtype=jnp.float32), 'ws3': jax.random.normal(ks[7], (DIM, N_SHARED * INTER), dtype=jnp.float32) * s(DIM), 'bs3': jnp.zeros((N_SHARED * INTER,), dtype=jnp.float32)}
        return inp
    _L0_ffn_all = _L0_ffn_setup()
    _L0_ffn_in = {k: v for k, v in _L0_ffn_all.items() if k in ('gate_w', 'gate_b', 'We1', 'be1', 'We2', 'be2', 'We3', 'be3', 'ws1', 'bs1', 'ws2', 'bs2', 'ws3', 'bs3')}
    del _L0_ffn_all
    return {'x': x, 'ctx_1024': ctx_1024, 'L0_attn_Wqkv': _L0_attn_in['Wqkv'], 'L0_attn_Wo': _L0_attn_in['Wo'], 'L0_attn_bo': _L0_attn_in['bo'], 'L0_xattn_Wq': _L0_xattn_in['Wq'], 'L0_xattn_Wk': _L0_xattn_in['Wk'], 'L0_xattn_Wv': _L0_xattn_in['Wv'], 'L0_xattn_Wo': _L0_xattn_in['Wo'], 'L0_ffn_gate_w': _L0_ffn_in['gate_w'], 'L0_ffn_gate_b': _L0_ffn_in['gate_b'], 'L0_ffn_We1': _L0_ffn_in['We1'], 'L0_ffn_be1': _L0_ffn_in['be1'], 'L0_ffn_We2': _L0_ffn_in['We2'], 'L0_ffn_be2': _L0_ffn_in['be2'], 'L0_ffn_We3': _L0_ffn_in['We3'], 'L0_ffn_be3': _L0_ffn_in['be3'], 'L0_ffn_ws1': _L0_ffn_in['ws1'], 'L0_ffn_bs1': _L0_ffn_in['bs1'], 'L0_ffn_ws2': _L0_ffn_in['ws2'], 'L0_ffn_bs2': _L0_ffn_in['bs2'], 'L0_ffn_ws3': _L0_ffn_in['ws3'], 'L0_ffn_bs3': _L0_ffn_in['bs3']}

def reference(x, ctx_1024, L0_attn_Wqkv, L0_attn_Wo, L0_attn_bo, L0_xattn_Wq, L0_xattn_Wk, L0_xattn_Wv, L0_xattn_Wo, L0_ffn_gate_w, L0_ffn_gate_b, L0_ffn_We1, L0_ffn_be1, L0_ffn_We2, L0_ffn_be2, L0_ffn_We3, L0_ffn_be3, L0_ffn_ws1, L0_ffn_bs1, L0_ffn_ws2, L0_ffn_bs2, L0_ffn_ws3, L0_ffn_bs3):
    import jax
    import jax.numpy as jnp

    def _L0_attn_ref(x, Wqkv, Wo, bo):
        import jax, jax.numpy as jnp
        import numpy as np
        DIM = 128
        NUM_HEADS = 16
        DIM_HEAD = 64
        POOL = 8
        SCALE = DIM_HEAD ** (-0.5)
        b, t, _ = x.shape
        h, d = (NUM_HEADS, DIM_HEAD)
        qkv = x @ Wqkv
        qkv = qkv.reshape(b, t, 3, h, d)
        qkv = jnp.transpose(qkv, (2, 0, 3, 1, 4))
        q, k, v = (qkv[0], qkv[1], qkv[2])
        agent = q.reshape(b, h, POOL, t // POOL, d).mean(axis=3)
        s1 = jnp.einsum('bhid,bhjd->bhij', agent * SCALE, k)
        p1 = jax.nn.softmax(s1, axis=-1)
        v_agent = jnp.einsum('bhij,bhjd->bhid', p1, v)
        s2 = jnp.einsum('bhid,bhjd->bhij', q * SCALE, agent)
        p2 = jax.nn.softmax(s2, axis=-1)
        out = jnp.einsum('bhij,bhjd->bhid', p2, v_agent)
        out = jnp.transpose(out, (0, 2, 1, 3)).reshape(b, t, h * d)
        return out @ Wo + bo

    def _L0_xattn_ref(query, key, value, Wq, Wk, Wv, Wo):
        import jax, jax.numpy as jnp
        import numpy as np
        N_HEADS = 16
        D_MODEL = 128
        D_K = D_MODEL // N_HEADS
        NEG_INF = -1000000000.0

        def _split_heads(x):
            B, S, _ = x.shape
            return x.reshape(B, S, N_HEADS, D_K).transpose(0, 2, 1, 3)
        B, S, D = query.shape
        Q = _split_heads(query @ Wq.T)
        K = _split_heads(key @ Wk.T)
        V = _split_heads(value @ Wv.T)
        scores = jnp.einsum('bhqd,bhkd->bhqk', Q, K) / jnp.sqrt(jnp.float32(D_K))
        causal = jnp.where(jnp.tril(jnp.ones((S, S), dtype=bool)), 0.0, NEG_INF).astype(scores.dtype)
        scores = scores + causal[None, None, :, :]
        attn = jax.nn.softmax(scores, axis=-1)
        heads = jnp.einsum('bhqk,bhkd->bhqd', attn, V)
        concat = heads.transpose(0, 2, 1, 3).reshape(B, S, D)
        out = concat @ Wo.T
        return out

    def _L0_ffn_ref(x, gate_w, gate_b, We1, be1, We2, be2, We3, be3, ws1, bs1, ws2, bs2, ws3, bs3):
        import jax, jax.numpy as jnp
        import numpy as np
        DIM = 128
        E = 16
        TOPK = 2
        G = 4
        TOPK_G = 2
        INTER = 64
        N_SHARED = 2
        ROUTE_SCALE = 1.0

        def _gate(xf, gate_w, gate_b):
            scores = xf @ gate_w.T
            scores = jax.nn.softmax(scores.astype(jnp.float32), axis=-1)
            orig = scores
            scores = scores + gate_b
            T = xf.shape[0]
            sg = scores.reshape(T, G, E // G)
            group_scores = jax.lax.top_k(sg, 2)[0].sum(-1)
            _, gidx = jax.lax.top_k(group_scores, TOPK_G)
            keep = jax.nn.one_hot(gidx, G).sum(axis=1) > 0
            sg = jnp.where(keep[:, :, None], sg, -jnp.inf)
            scores = sg.reshape(T, E)
            _, idx = jax.lax.top_k(scores, TOPK)
            weights = jnp.take_along_axis(orig, idx, axis=1)
            weights = (weights * ROUTE_SCALE).astype(xf.dtype)
            return (weights, idx)
        shape = x.shape
        xf = x.reshape(-1, DIM)
        weights, idx = _gate(xf, gate_w, gate_b)
        combine = (jax.nn.one_hot(idx, E, dtype=xf.dtype) * weights[..., None]).sum(1)
        h1 = jnp.einsum('td,edi->tei', xf, We1) + be1
        h3 = jnp.einsum('td,edi->tei', xf, We3) + be3
        h = jax.nn.silu(h1) * h3
        yo = jnp.einsum('tei,eid->ted', h, We2) + be2
        y = jnp.einsum('te,ted->td', combine, yo)
        z = jax.nn.silu(xf @ ws1 + bs1) * (xf @ ws3 + bs3) @ ws2 + bs2
        return (y + z).reshape(shape)
    x = x + _L0_attn_ref(_layernorm(x, axis=-1), L0_attn_Wqkv, L0_attn_Wo, L0_attn_bo)
    x = x + _L0_xattn_ref(_layernorm(x, axis=-1), ctx_1024, ctx_1024, L0_xattn_Wq, L0_xattn_Wk, L0_xattn_Wv, L0_xattn_Wo)
    x = x + _L0_ffn_ref(_layernorm(x, axis=-1), L0_ffn_gate_w, L0_ffn_gate_b, L0_ffn_We1, L0_ffn_be1, L0_ffn_We2, L0_ffn_be2, L0_ffn_We3, L0_ffn_be3, L0_ffn_ws1, L0_ffn_bs1, L0_ffn_ws2, L0_ffn_bs2, L0_ffn_ws3, L0_ffn_bs3)
    return x

_drawn_inputs = setup_inputs


def setup_inputs(seed=0):
    import zlib

    import numpy as np

    out = dict(_drawn_inputs(seed))
    spreads = {'L0_ffn_gate_b': (0.0, 0.1),
     'L0_ffn_be1': (0.0, 0.636),
     'L0_ffn_be2': (0.0, 0.412),
     'L0_ffn_be3': (0.0, 0.661),
     'L0_ffn_bs1': (0.0, 0.1),
     'L0_ffn_bs2': (0.0, 0.1),
     'L0_ffn_bs3': (0.0, 0.1)}
    factors = {'L0_attn_bo': 4.568}
    for name, (base, spread) in spreads.items():
        noise = np.random.default_rng([zlib.crc32(name.encode()), seed]).standard_normal(out[name].shape)
        drawn = base * np.exp(spread * noise) if base else spread * noise
        out[name] = jnp.asarray(drawn.astype(out[name].dtype))
    for name, factor in factors.items():
        out[name] = (out[name] * factor).astype(out[name].dtype)
    return out
```

```python
import numpy as np
import concourse.bass as bass
from concourse import mybir
from contextlib import ExitStack


def decoder_block(nc, x, ctx_in, Wqkv, Wo_a, bo, Wq, Wk, Wv, Wo_x, gate_w, gate_b,
                  We1, be1, We2, be2, We3, be3, ws1, bs1, ws2, bs2, ws3, bs3, out):
    fp32, bf16 = mybir.dt.float32, mybir.dt.bfloat16
    ALU, ACT, AX = mybir.AluOpType, mybir.ActivationFunctionType, mybir.AxisListType.X

    B, S, D = x.shape
    P = 128
    GB = 16
    GROUPS = B // GB
    TOK = GB * S
    T = TOK // P
    QT = 4
    Q = T // QT
    H, POOL, DH = 16, 8, 64
    HI = H * POOL
    XH, XC = 16, 8
    HALF = XH // 2
    E, EG, EI = 16, 4, 64
    EP = E // 2
    CH = 512
    CHUNKS = TOK // CH
    EPS = 1e-5
    AGENT_SCALE = DH ** -0.5 / (S // POOL)
    X_SCALE = XC ** -0.5
    MASKED = -1e9 / X_SCALE
    FAR, FARTHER = 1e30, 1e32

    x_v = x.rearrange("(g b) s d -> g (b s) d", b=GB).rearrange("g (t p) d -> g p t d", p=P)
    c_v = ctx_in.rearrange("(g b) s d -> g (b s) d", b=GB).rearrange("g (t p) d -> g p t d", p=P)
    o_v = out.rearrange("(g b) s d -> g (b s) d", b=GB).rearrange("g (t p) d -> g p t d", p=P)

    main = ["xnT1", "ctxT", "KT", "V0", "V1", "M0", "M1", "M2", "M3",
            "s1_0", "s2_0", "s1_1", "s2_1", "p1T0", "p2T0", "PX0", "p1T1", "p2T1", "PX1",
            "UT0", "UT1", "U0", "U1", "xnT2", "QT", "S0", "S1"]
    for t in range(T):
        main.append(f"PT{t}")
        if t + 2 < T:
            main.append(f"S{t + 2}")
    main += ["xnT3", "gate"]
    main += [f"H0_{EP}", "combT", "combS"]
    main += [f"H0_{p}" for p in range(EP)] + [f"H1_{EP}"] + [f"H1_{p}" for p in range(EP)]
    side = [f"OL{t}" for t in range(T)] + [f"C{c}_{p}" for c in range(CHUNKS) for p in range(EP)]
    rows = [f"Ya{q}" for q in range(Q)] + [f"Yx{q}" for q in range(Q)] + [f"Ym{c}" for c in range(CHUNKS)]
    RINGS = {"main": (main, 3), "side": (side, 1), "rows": (rows, 1)}
    place = {}
    for ring, (names, n) in RINGS.items():
        for at, name in enumerate(names):
            k = at % n
            place[name] = (ring, k, at // n, len(range(k, len(names), n)))

    with ExitStack() as ctx:
        def sb(name, shape, dt=fp32):
            return ctx.enter_context(nc.sbuf_tensor(name, shape, dt))

        def sem(name):
            return ctx.enter_context(nc.semaphore(name))

        Kx = sb("Kx", [P, XH, TOK])
        wqkv = Kx[:, 0:3, :].rearrange("p a n -> p (a n)")
        wT = Kx[:, 3:6, :].rearrange("p a (b n) -> p (a b) n", n=P)
        woa = Kx[:, 6:7, :].rearrange("p a (b n) -> p (a b) n", n=D)
        xw = Kx[:, 7, 0:512].rearrange("p (a n) -> p a n", n=D)
        gw = Kx[0:E, 7, 512:512 + D]
        A1 = sb("A1", [P, H, D])
        A2 = sb("A2", [P, H, D])
        Wvo = sb("Wvo", [P, H, D])
        xwT = sb("xwT", [P, 4, D])
        woM = sb("woM", [P, 2, 2, D])
        w1 = sb("w1", [P, E + 2, EI])
        w3 = sb("w3", [P, E + 2, EI])
        w2 = sb("w2", [P, EP + 1, D])
        b1 = sb("b1", [P, EP + 1])
        b3 = sb("b3", [P, EP + 1])
        b2x = sb("b2x", [P, D])
        gwT = sb("gwT", [P, E])
        gb = sb("gb", [P, E])
        bo_b = sb("bo_b", [P, D])
        ident = sb("ident", [P, P])
        identb = sb("identb", [P, P], bf16)
        maskb = sb("maskb", [P, HALF, S], bf16)
        parity = sb("parity", [P, XH, XC])
        bones = sb("bones", [P, 2, 2, XC])
        onehot3 = sb("onehot3", [P, E], bf16)
        spread = sb("spread", [P, EP, 2, EI], bf16)
        lower = sb("lower", [P, EG, EG])
        down = sb("down", [P, E])
        mhalf = sb("mhalf", [P, T])
        xin = sb("xin", [P, T, D])
        cin = sb("cin", [P, T, D])
        xr = sb("xr", [P, T, D])
        xn = sb("xn", [P, T, D])
        xo = xn
        xnT = sb("xnT", [P, TOK + S])
        stats = sb("stats", [P, T, 6])
        mean, mean2, diff, diff2, sqd, sqd2 = [sb(f"norm{k}", [P, T]) for k in range(6)]
        ve = sb("ve", [P, T])
        rstd = sb("rstd", [P, T])
        pooled = sb("pooled", [P, GB * POOL])
        M = sb("M", [P, 2, GB, HI])
        e1 = sb("e1", [P, 8, S])
        m1 = sb("m1", [P, 8])
        l1 = sb("l1", [P, 8])
        r1 = sb("r1", [P, GB])
        e2 = sb("e2", [P, QT, HI])
        m2 = sb("m2", [P, QT * H])
        l2 = sb("l2", [P, QT * H])
        r2 = sb("r2", [P, QT * H])
        p1T = sb("p1T", [P, QT, 2, HI])
        p2T = sb("p2T", [P, TOK])
        PX = sb("PX", [P, GB, HI])
        UT = sb("UT", [P, GB, HI])
        U = sb("U", [P, GB, D])
        ctxT = sb("ctxT", [P, TOK])
        KT = p2T
        QTs = ctxT
        Vb = sb("Vb", [P, T, XH // 2, 2, 2 * XC])
        mx = sb("mx", [P, 2, XH])
        pr = M[:, 0].rearrange("p b h -> p (b h)").rearrange("p (k h s) -> p k h s", k=2, s=S)
        pT = M[:, 1].rearrange("p b h -> p (b h)").rearrange("p (k j q) -> p k j q", k=2, q=P)
        rl = sb("rl", [P, 2, P])
        On = sb("On", [P, 2, 2, P])
        g1 = sb("g1", [P, T])
        g2 = sb("g2", [P, T])
        gs = sb("gs", [P, T * EG])
        rank = sb("rank", [P, T * EG])
        keep = sb("keep", [P, T * EG])
        kb = sb("kb", [P, T * EG])
        TE = T * E
        ga, gex, orig, sc = [p2T[:, TE * k:TE * k + TE].rearrange("p (t e) -> p t e", e=E) for k in range(4)]
        gta, gtb = [p2T[:, TE * k:TE * k + TE].rearrange("p (t a b) -> p t a b", a=EG, b=EG) for k in (4, 5)]
        ps6 = p2T[:, TE * 6:TE * 6 + T * EG * 6].rearrange("p (k n) -> p k n", n=6)
        tv = e2[:, 0, :].rearrange("p (t e) -> p t e", e=E)
        oh = e2[:, 1:3, :].rearrange("p k (t e) -> p k t e", e=E)
        comb = sb("comb", [P, T, P])
        combs = sb("combs", [P, T, P], bf16)
        flat = [a[:].rearrange("p b h -> p (b h)") for a in (PX, UT, U)]
        sil = flat[0][:, 0:2 * CH].rearrange("p (k n) -> p k n", k=2)
        hid = flat[0][:, 2 * CH:4 * CH].rearrange("p (k n) -> p k n", k=2)
        hT = flat[1][:, 0:2 * CH].rearrange("p (k n) -> p k n", k=2)
        combT = flat[1][:, 2 * CH:4 * CH]
        combsT = flat[2][:, 0:CH].bitcast(bf16)

        slot = [ctx.enter_context(nc.psum_tensor(f"slot{k}", [P, 1024], fp32)) for k in range(3)]
        side_b = ctx.enter_context(nc.psum_tensor("side_b", [P, 512], fp32))
        rows_b = ctx.enter_context(nc.psum_tensor("rows_b", [P, 512], fp32))
        bank = {"main": slot, "side": [side_b], "rows": [rows_b]}

        full = {(r, k): sem(f"{r}{k}_full") for r, (_, n) in RINGS.items() for k in range(n)}

        loaded_w = sem("loaded_w")
        loaded_m = sem("loaded_m")
        const_step = sem("const_step")
        consts = sem("consts")
        setup_ps = sem("setup_ps")
        setup_cp = sem("setup_cp")
        weights_up = sem("weights_up")
        spread_wo = sem("spread_wo")
        x_loaded = sem("x_loaded")
        c_loaded = sem("c_loaded")
        xr_ready = sem("xr_ready")
        var_ready = sem("var_ready")
        rstd_ready = sem("rstd_ready")
        xn_ready = sem("xn_ready")
        xnT_ready = sem("xnT_ready")
        ctxT_ready = sem("ctxT_ready")
        KT_ready = sem("KT_ready")
        Kx_ready = sem("Kx_ready")
        V_ready = sem("V_ready")
        pooled_ready = sem("pooled_ready")
        Ma_ready = sem("Ma_ready")
        Md_ready = sem("Md_ready")
        d1_ready = sem("d1_ready")
        d2_ready = sem("d2_ready")
        e1_ready = sem("e1_ready")
        e2_ready = sem("e2_ready")
        p2_ready = sem("p2_ready")
        p1T_ready = sem("p1T_ready")
        p2T_ready = sem("p2T_ready")
        PX_ready = sem("PX_ready")
        UT_ready = sem("UT_ready")
        U_ready = sem("U_ready")
        QT_ready = sem("QT_ready")
        dx_ready = sem("dx_ready")
        pr_ready = sem("pr_ready")
        pT_ready = sem("pT_ready")
        On_ready = sem("On_ready")
        dg_ready = sem("dg_ready")
        gex_ready = sem("gex_ready")
        comb_ready = sem("comb_ready")
        combT_ready = sem("combT_ready")
        sil_ready = sem("sil_ready")
        hid_ready = sem("hid_ready")
        attn_added = sem("attn_added")
        xattn_added = sem("xattn_added")
        hT_ready = sem("hT_ready")
        out_ready = sem("out_ready")
        stored = sem("stored")
        vec = sem("vec")

        VEC_LINKS = 67

        block = ctx.enter_context(nc.Block())

        order = [EP] + list(range(EP))

        def n_of(c, n):
            return (EP + 1) * c + n

        def ps(name):
            ring, k, _, _ = place[name]
            return bank[ring][k]

        HS = (EP + 1) * CHUNKS
        read = {"xnT1": (xnT_ready, 3, 0), "xnT2": (xnT_ready, 3, 1), "xnT3": (xnT_ready, 3, 2),
                "ctxT": (ctxT_ready, 1, 0), "KT": (KT_ready, 1, 0), "QT": (QT_ready, 1, 0), "gate": (dg_ready, 1, 0),
                "M0": (Ma_ready, 2, 0), "M1": (Md_ready, 2, 0), "M2": (Ma_ready, 2, 1), "M3": (Md_ready, 2, 1),
                "combT": (combT_ready, 2, 0), "combS": (combT_ready, 2, 1)}
        for n in range(2):
            read |= {f"V{n}": (V_ready, 2, n), f"UT{n}": (UT_ready, 2, n), f"U{n}": (U_ready, 2, n)}
        for q in range(Q):
            read |= {f"s1_{q}": (d1_ready, Q, q), f"s2_{q}": (d2_ready, Q, q), f"p1T{q}": (p1T_ready, Q, q),
                     f"p2T{q}": (p2T_ready, Q, q), f"PX{q}": (PX_ready, Q, q), f"Ya{q}": (attn_added, Q, q),
                     f"Yx{q}": (xattn_added, Q, q)}
        for t in range(T):
            read |= {f"S{t}": (dx_ready, T, t), f"PT{t}": (pT_ready, T, t), f"OL{t}": (On_ready, T, t)}
        for c in range(CHUNKS):
            read |= {f"H{c}_{EP}": (hT_ready, HS, (EP + 1) * c), f"Ym{c}": (out_ready, CHUNKS, c)}
            for p in range(EP):
                read |= {f"H{c}_{p}": (hid_ready, EP * CHUNKS, EP * c + p),
                         f"C{c}_{p}": (hT_ready, HS, (EP + 1) * c + p + 1)}

        def wait_free(pe, g, name):
            ring, k, use, _ = place[name]
            if use:
                before = RINGS[ring][0][RINGS[ring][1] * (use - 1) + k]
                signal, per, n = read[before]
                pe.wait_ge(signal, g * per + n + 1)
            elif ring == "rows":
                pe.wait_ge(out_ready, CHUNKS * g)
            else:
                pe.wait_ge(hT_ready, HS * g)

        def wait_full(eng, g, name):
            ring, k, use, per = place[name]
            eng.wait_ge(full[ring, k], g * per + use + 1)

        def fulled(name):
            return full[place[name][:2]]

        SETUP = [("T", s) for s in range(3)] + [("W", s) for s in range(6)] + [("X", 0)]

        @block.sync
        def _(sp):
            sp.dma_start(wqkv, Wqkv).then_inc(loaded_w, 16)
            sp.dma_start(woa, Wo_a.rearrange("(b p) d -> p b d", p=P)).then_inc(loaded_w, 16)
            for n, w in enumerate((Wq, Wk, Wv, Wo_x)):
                sp.dma_start(xw[:, n, :], w).then_inc(loaded_w, 16)
            sp.dma_start(gw, gate_w).then_inc(loaded_w, 16)
            sp.dma_start(gb[:], gate_b.partition_broadcast(P)).then_inc(loaded_m, 16)
            sp.dma_start(bo_b[:], bo.partition_broadcast(P)).then_inc(loaded_m, 16)
            for w_sb, we, ws in ((w1, We1, ws1), (w3, We3, ws3)):
                sp.dma_start(w_sb[:, 0:E, :], we.rearrange("e d i -> d e i")).then_inc(loaded_m, 16)
                sp.dma_start(w_sb[:, E:E + 2, :], ws.rearrange("d (e i) -> d e i", i=EI)).then_inc(loaded_m, 16)
            sp.dma_start(w2[:, 0:EP, :], We2.rearrange("(p a) i d -> (a i) p d", a=2)).then_inc(loaded_m, 16)
            sp.dma_start(w2[:, EP, :], ws2).then_inc(loaded_m, 16)
            with nc.allow_non_contiguous_dma("biases, a column each, once"):
                for b_sb, be, bs in ((b1, be1, bs1), (b3, be3, bs3)):
                    sp.dma_start(b_sb[:, 0:EP], be.rearrange("(p a) i -> (a i) p", a=2)).then_inc(loaded_m, 16)
                    sp.dma_start(b_sb[:, EP:EP + 1], bs.rearrange("(p a) -> p a", a=1)).then_inc(loaded_m, 16)
            sp.wait_ge(consts, 1)
            sp.dma_start(b2x[0:E, :], be2).then_inc(loaded_m, 16)
            sp.dma_start(b2x[E:E + 1, :], bs2.rearrange("(a d) -> a d", a=1)).then_inc(loaded_m, 16)
            sp.wait_ge(setup_cp, len(SETUP))
            for s in range(2):
                for b in range(2):
                    for gq in range(4):
                        sp.dma_start(woM[32 * gq + 16 * b:32 * gq + 16 * b + 16, s, b, :],
                                     xwT[64 * s + 16 * gq:64 * s + 16 * gq + 16, 3, :]).then_inc(spread_wo, 16)
            sp.wait_ge(consts, 3)
            with sp.Fori(0, GROUPS) as g:
                sp.wait_ge(xn_ready, 3 * g)
                sp.dma_start(xin[:], x_v[bass.ds(g, 1)].rearrange("a p t d -> (a p) t d")).then_inc(x_loaded, 16)
                sp.wait_ge(pr_ready, T * g)
                sp.dma_start(cin[:], c_v[bass.ds(g, 1)].rearrange("a p t d -> (a p) t d")).then_inc(c_loaded, 16)
                sp.wait_ge(KT_ready, g + 1)
                for h in range(XH):
                    sp.dma_start(Kx[XC * h:XC * h + XC, h, :], KT[XC * h:XC * h + XC, :]).then_inc(Kx_ready, 16)

        @block.gpsimd
        def _(pool):
            steps = [0]

            def step(ins):
                steps[0] += 1
                ins.then_inc(const_step, 1)
                pool.wait_ge(const_step, steps[0])

            step(nc.gpsimd.memset(b2x[:], 0.0))
            nc.gpsimd.memset(mhalf[:], -0.5).then_inc(consts, 1)
            nc.gpsimd.memset(woM[:], 0.0)
            nc.gpsimd.memset(p1T[:], 0.0)
            nc.gpsimd.memset(xnT[:, TOK:TOK + S], 0.0)
            nc.gpsimd.memset(combs[:], 0.0)
            nc.gpsimd.memset(comb[:], 0.0)
            nc.gpsimd.memset(ident[:], 0.0)
            nc.gpsimd.memset(onehot3[:], 0.0)
            nc.gpsimd.memset(maskb[:], 0.0)
            nc.gpsimd.memset(lower[:], 1.0)
            nc.gpsimd.memset(parity[:], 0.0)
            step(nc.gpsimd.memset(bones[:], 0.0))
            nc.gpsimd.memset(comb[:, :, E:E + 1], 1.0)
            nc.gpsimd.iota(down[:], pattern=[[-1, E]], base=E, channel_multiplier=0,
                           allow_small_or_imprecise_dtypes=True)
            step(nc.gpsimd.affine_select(out=ident[:], in_=ident[:], compare_op=ALU.not_equal, fill=1.0, base=0,
                                         pattern=[[-1, P]], channel_multiplier=1))
            for k in range(3):
                step(nc.gpsimd.affine_select(out=onehot3[:], in_=onehot3[:], compare_op=ALU.not_equal, fill=1.0,
                                             base=-E * k, pattern=[[-1, E]], channel_multiplier=1))
            step(nc.gpsimd.affine_select(out=lower[:], in_=lower[:], compare_op=ALU.is_gt, fill=0.0, base=0,
                                         pattern=[[1, EG], [-1, EG]], channel_multiplier=0))
            for r in range(2):
                rr = slice(64 * r, 64 * r + 64)
                step(nc.gpsimd.affine_select(out=maskb[rr], in_=maskb[rr], compare_op=ALU.is_ge, fill=MASKED, base=0,
                                             pattern=[[0, HALF], [-1, S]], channel_multiplier=1))
                step(nc.gpsimd.memset(parity[rr].rearrange("p (j a) c -> p j a c", a=2)[:, :, r, :], 1.0))
                step(nc.gpsimd.memset(bones[rr, :, r, :], 1.0))
            nc.gpsimd.tensor_copy(identb[:], ident[:]).then_inc(const_step, 1)
            steps[0] += 1
            nc.gpsimd.tensor_copy(spread[:].rearrange("r p a i -> r (p a) i"),
                                  onehot3[:].unsqueeze(2).to_broadcast([P, E, EI])).then_inc(const_step, 1)
            steps[0] += 1
            pool.wait_ge(const_step, steps[0])
            nc.gpsimd.memset(mhalf[:], -0.5).then_inc(consts, 1)
            pool.wait_ge(consts, 2)
            pool.wait_ge(setup_cp, len(SETUP))
            nc.gpsimd.memset(Kx[:], 0.0).then_inc(consts, 1)
            pool.wait_ge(loaded_m, 16 * 14)
            with pool.Fori(0, GROUPS) as g:
                pool.wait_ge(x_loaded, 16 * g + 16)
                pool.wait_ge(out_ready, Q * g)
                nc.gpsimd.tensor_tensor(xr[:], xin[:], bo_b[:].unsqueeze(1).to_broadcast([P, T, D]),
                                        ALU.add).then_inc(xr_ready, 1)
                for n in range(3):
                    pool.wait_ge(var_ready, 3 * g + n + 1)
                    nc.gpsimd.tensor_tensor(rstd[:], ve[:], mhalf[:], ALU.pow).then_inc(rstd_ready, 1)
                for q in range(Q):
                    pool.wait_ge(out_ready, Q * g + q + 1)
                    pool.dma_start(o_v[bass.ds(g, 1)].rearrange("a p t d -> (a p) t d")[:, QT * q:QT * q + QT, :],
                                   xo[:, QT * q:QT * q + QT, :]).then_inc(stored, 16)
            pool.wait_ge(stored, 16 * Q * GROUPS)

        @block.tensor
        def _(pe):
            mm = nc.tensor.matmul
            pe.wait_ge(consts, 2)
            pe.wait_ge(loaded_w, 16 * 7)
            for n, (kind, s) in enumerate(SETUP):
                dst = slot[n % 3]
                if n >= 3:
                    pe.wait_ge(setup_cp, n - 2)
                if kind == "T":
                    for k in range(8):
                        c0 = (8 * s + k) * P
                        last = nc.tensor.transpose(dst[:, P * k:P * k + P], wqkv[:, c0:c0 + P], ident[:])
                elif kind == "W":
                    if s == 0:
                        pe.wait_ge(setup_cp, 3)
                    for k in range(8):
                        h = 8 * (s % 2) + k
                        rr = slice(64 * (h % 2), 64 * (h % 2) + 64)
                        a = (wT[rr, h // 2, :], wT[rr, h // 2, :], wT[rr, 16 + h // 2, :])[s // 2]
                        b = (wT[rr, 8 + h // 2, :], wT[rr, h // 2, :], woa[rr, h // 2, :])[s // 2]
                        c0 = 512 * (h % 2) + P * (k // 2)
                        last = mm(dst[:, c0:c0 + P], a, b, start=True, stop=True)
                else:
                    for k in range(4):
                        nc.tensor.transpose(dst[:, P * k:P * k + P], xw[:, k, :], ident[:])
                    last = nc.tensor.transpose(dst[:, 512:512 + E], gw, ident[0:E, 0:E])
                last.then_inc(setup_ps, 1)
            pe.wait_ge(setup_cp, len(SETUP))
            pe.wait_ge(spread_wo, 16 * 16)
            pe.wait_ge(loaded_m, 16 * 14)

            with pe.Fori(0, GROUPS) as g:
                def transposes(name, src):
                    wait_free(pe, g, name)
                    for t in range(T):
                        last = nc.tensor.transpose(ps(name)[:, P * t:P * t + P], src[:, t, :], ident[:])
                    last.then_inc(fulled(name), 1)

                pe.wait_ge(xn_ready, 3 * g + 1)
                transposes("xnT1", xn)
                pe.wait_ge(c_loaded, 16 * g + 16)
                transposes("ctxT", cin)
                pe.wait_ge(ctxT_ready, g + 1)
                wait_free(pe, g, "KT")
                for c in range(2):
                    last = mm(ps("KT")[:, 512 * c:512 * c + 512], xwT[:, 1, :], ctxT[:, 512 * c:512 * c + 512],
                              start=True, stop=True)
                last.then_inc(fulled("KT"), 1)
                for v in range(2):
                    wait_free(pe, g, f"V{v}")
                    for k in range(8):
                        b = 8 * v + k
                        for r in range(2):
                            last = mm(ps(f"V{v}")[64 * r:64 * r + 64, P * k:P * k + P], ctxT[:, S * b:S * b + S],
                                      xwT[:, 2, :], start=True, stop=True)
                    last.then_inc(fulled(f"V{v}"), 1)
                pe.wait_ge(pooled_ready, g + 1)
                for n in range(4):
                    wait_free(pe, g, f"M{n}")
                    for k in range(8):
                        A = A1 if n < 2 else A2
                        last = mm(ps(f"M{n}")[:, P * k:P * k + P], A[:, 8 * (n % 2) + k, :], pooled[:],
                                  start=True, stop=True)
                    last.then_inc(fulled(f"M{n}"), 1)
                pe.wait_ge(Ma_ready, 2 * g + 2)
                pe.wait_ge(Md_ready, 2 * g + 2)
                for q in range(Q):
                    if place[f"s1_{q}"][2] > place["M3"][2] + 1:
                        wait_free(pe, g, f"s1_{q}")
                    for k in range(8):
                        b = 8 * q + k
                        last = mm(ps(f"s1_{q}")[:, P * k:P * k + P], M[:, 0, b, :], xnT[:, S * b:S * b + P],
                                  start=True, stop=True)
                    last.then_inc(fulled(f"s1_{q}"), 1)
                    if q:
                        wait_free(pe, g, f"s2_{q}")
                    for k in range(8):
                        b, r = 8 * q + k, k % 2
                        last = mm(ps(f"s2_{q}")[64 * r:64 * r + 64, P * (k // 2):P * (k // 2) + P],
                                  xnT[:, S * b:S * b + S], M[:, 1, b, :], start=True, stop=True)
                    last.then_inc(fulled(f"s2_{q}"), 1)
                for q in range(Q):
                    wait_free(pe, g, f"p1T{q}")
                    pe.wait_ge(e1_ready, Q * g + q + 1)
                    for t in range(QT):
                        last = nc.tensor.transpose(ps(f"p1T{q}")[:, P * t:P * t + P],
                                                   e1[:, 2 * t:2 * t + 2, :].rearrange("p b s -> p (b s)"), ident[:])
                    last.then_inc(fulled(f"p1T{q}"), 1)
                    wait_free(pe, g, f"p2T{q}")
                    pe.wait_ge(p2_ready, Q * g + q + 1)
                    for t in range(QT):
                        last = nc.tensor.transpose(ps(f"p2T{q}")[:, P * t:P * t + P], e2[:, t, :], ident[:])
                    last.then_inc(fulled(f"p2T{q}"), 1)
                    wait_free(pe, g, f"PX{q}")
                    pe.wait_ge(p1T_ready, Q * g + q + 1)
                    for t in range(QT):
                        last = mm(ps(f"PX{q}")[:, 256 * t:256 * t + 256], xn[:, QT * q + t, :],
                                  p1T[:, t, :, :], start=True, stop=True)
                    last.then_inc(fulled(f"PX{q}"), 1)
                pe.wait_ge(PX_ready, Q * g + Q)
                for n in range(2):
                    wait_free(pe, g, f"UT{n}")
                    for k in range(8):
                        h = 8 * n + k
                        last = mm(ps(f"UT{n}")[:, P * k:P * k + P], Wvo[:, h, :],
                                  PX[:, :, POOL * h:POOL * h + POOL], start=True, stop=True)
                    last.then_inc(fulled(f"UT{n}"), 1)
                pe.wait_ge(UT_ready, 2 * g + 2)
                for n in range(2):
                    wait_free(pe, g, f"U{n}")
                    for k in range(8):
                        last = nc.tensor.transpose(ps(f"U{n}")[:, P * k:P * k + P], UT[:, 8 * n + k, :], ident[:])
                    last.then_inc(fulled(f"U{n}"), 1)
                pe.wait_ge(p2T_ready, Q * g + Q)
                for q in range(Q):
                    pe.wait_ge(U_ready, Q * g + q + 1)
                    wait_free(pe, g, f"Ya{q}")
                    for k in range(8):
                        b, r = 8 * q + k, k % 2
                        last = mm(ps(f"Ya{q}")[64 * r:64 * r + 64, P * (k // 2):P * (k // 2) + P],
                                  p2T[:, S * b:S * b + S], U[:, b, :], start=True, stop=True)
                    last.then_inc(fulled(f"Ya{q}"), 1)

                pe.wait_ge(xn_ready, 3 * g + 2)
                transposes("xnT2", xn)
                wait_free(pe, g, "QT")
                pe.wait_ge(xnT_ready, 3 * g + 2)
                for c in range(2):
                    last = mm(ps("QT")[:, 512 * c:512 * c + 512], xwT[:, 0, :], xnT[:, 512 * c:512 * c + 512],
                              start=True, stop=True)
                last.then_inc(fulled("QT"), 1)
                pe.wait_ge(QT_ready, g + 1)
                pe.wait_ge(Kx_ready, 16 * XH * g + 16 * XH)
                pe.wait_ge(V_ready, 2 * g + 2)

                def scores(t):
                    name = f"S{t}"
                    wait_free(pe, g, name)
                    for hh in range(2):
                        dst = ps(name)[:, 512 * hh:512 * hh + 512]
                        mm(dst, identb[:], maskb[:].rearrange("p h s -> p (h s)"), start=True, stop=False,
                           skip_group_check=True)
                        for r in range(2):
                            b = 2 * t + r
                            last = mm(dst[64 * r:64 * r + 64, :], QTs[:, S * b:S * b + S],
                                      Kx[:, HALF * hh:HALF * hh + HALF, S * b:S * b + S], start=False, stop=True,
                                      skip_group_check=True)
                    last.then_inc(fulled(name), 1)

                def turn(t):
                    name = f"PT{t}"
                    wait_free(pe, g, name)
                    pe.wait_ge(pr_ready, T * g + t + 1)
                    src = pr[:, t % 2, :, :].rearrange("p h s -> p (h s)")
                    for j in range(8):
                        last = nc.tensor.transpose(ps(name)[:, P * j:P * j + P], src[:, P * j:P * j + P], ident[:])
                    last.then_inc(fulled(name), 1)

                def values(t):
                    name = f"OL{t}"
                    wait_free(pe, g, name)
                    pe.wait_ge(pT_ready, T * g + t + 1)
                    for j in range(8):
                        gq, s = j % 4, j // 4
                        rr = slice(32 * gq, 32 * gq + 32)
                        mm(ps(name)[rr, P * s:P * s + P], Vb[:, t, j, :, :].rearrange("p a c -> p (a c)"),
                           pT[:, t % 2, j, :], start=True, stop=True, tile_position=(0, 32 * gq))
                        last = mm(ps(name)[rr, 256 + P * s:256 + P * s + P], bones[:].rearrange("p a b c -> p (a b c)"),
                                  pT[:, t % 2, j, :], start=True, stop=True, tile_position=(0, 32 * gq))
                    last.then_inc(fulled(name), 1)

                def project(t):
                    name = f"Yx{t // QT}"
                    if t % QT == 0:
                        wait_free(pe, g, name)
                    pe.wait_ge(On_ready, T * g + t + 1)
                    for r in range(2):
                        for s in range(2):
                            last = mm(ps(name)[64 * r:64 * r + 64, P * (t % QT):P * (t % QT) + P],
                                      On[:, t % 2, s, 64 * r:64 * r + 64], woM[:, s, r, :],
                                      start=(s == 0), stop=(s == 1))
                    if t % QT == QT - 1:
                        last.then_inc(fulled(name), 1)

                scores(0)
                scores(1)
                for t in range(T):
                    turn(t)
                    if t + 2 < T:
                        scores(t + 2)
                    values(t)
                    if t >= 1:
                        project(t - 1)
                project(T - 1)

                pe.wait_ge(xn_ready, 3 * g + 3)
                transposes("xnT3", xn)
                pe.wait_ge(xnT_ready, 3 * g + 3)
                wait_free(pe, g, "gate")
                for t in range(T):
                    last = mm(ps("gate")[:, E * t:E * t + E], xnT[:, P * t:P * t + P], gwT[:], start=True, stop=True)
                last.then_inc(fulled("gate"), 1)

                def up(c, p):
                    name = f"H{c}_{p}"
                    wait_free(pe, g, name)
                    for k, w in enumerate((w1, w3)):
                        last = mm(ps(name)[:, 512 * k:512 * k + 512], w[:, 2 * p:2 * p + 2, :],
                                  xnT[:, CH * c:CH * c + CH], start=True, stop=True)
                    last.then_inc(fulled(name), 1)

                def weights_of(c, p):
                    name = f"C{c}_{p}"
                    wait_free(pe, g, name)
                    mm(ps(name)[:], spread[:, p, :, :], combsT[:, CH * c:CH * c + CH], start=True,
                       stop=True).then_inc(fulled(name), 1)

                def down_to(c, n):
                    name = f"Ym{c}"
                    p = order[n]
                    if n == 0:
                        wait_free(pe, g, name)
                    pe.wait_ge(hT_ready, (EP + 1) * (CHUNKS * g + c) + n + 1)
                    for t in range(QT):
                        last = mm(ps(name)[:, P * t:P * t + P], hT[:, n % 2, P * t:P * t + P], w2[:, p, :],
                                  start=(n == 0 and t == 0), stop=False, skip_group_check=True)
                    return last

                up(0, EP)
                for name, src, idn, dst in (("combT", comb, ident, None), ("combS", combs, identb, None)):
                    wait_free(pe, g, name)
                    if name == "combT":
                        pe.wait_ge(comb_ready, g + 1)
                    dst = ps(name)[:] if name == "combT" else ps(name)[:, 0:512].bitcast(bf16)
                    for t in range(T):
                        last = nc.tensor.transpose(dst[:, P * t:P * t + P], src[:, t, :], idn[:])
                    last.then_inc(fulled(name), 1)
                pe.wait_ge(combT_ready, 2 * g + 2)
                for c in range(CHUNKS):
                    if c:
                        up(c, EP)
                    for p in range(EP):
                        up(c, p)
                        weights_of(c, p)
                        down_to(c, p)
                    down_to(c, EP)
                    for t in range(QT):
                        last = mm(ps(f"Ym{c}")[:, P * t:P * t + P], combT[:, CH * c + P * t:CH * c + P * t + P], b2x[:],
                                  start=False, stop=True, skip_group_check=True)
                    last.then_inc(fulled(f"Ym{c}"), 1)

        @block.scalar
        def _(act):
            cp = nc.scalar.copy
            for n, (kind, s) in enumerate(SETUP):
                act.wait_ge(setup_ps, n + 1)
                src = slot[n % 3][:].rearrange("p (k d) -> p k d", d=P)
                if kind == "T":
                    cp(wT[:, 8 * s:8 * s + 8, :], src).then_inc(setup_cp, 1)
                elif kind == "W":
                    dst = (A1, A2, Wvo)[s // 2]
                    cp(dst[:, 8 * (s % 2):8 * (s % 2) + 8, :].rearrange("p (k r) d -> p r k d", r=2),
                       src.rearrange("p (r k) d -> p r k d", r=2)).then_inc(setup_cp, 1)
                else:
                    cp(xwT[:], src[:, 0:4, :])
                    cp(gwT[:], slot[n % 3][:, 512:512 + E]).then_inc(setup_cp, 1)
            act.wait_ge(consts, 2)
            act.wait_ge(loaded_m, 16 * 14)

            with act.Fori(0, GROUPS) as g:
                def moved(name, dst, ready, src=None):
                    wait_full(act, g, name)
                    cp(dst, ps(name)[:] if src is None else src).then_inc(ready, 1)

                moved("xnT1", xnT[:, 0:TOK], xnT_ready)
                moved("ctxT", ctxT[:], ctxT_ready)
                moved("KT", KT[:], KT_ready)
                for n in (0, 2):
                    moved(f"M{n}", M[:, n // 2, :, 0:64].rearrange("p b (h i) -> p h b i", i=POOL), Ma_ready,
                          ps(f"M{n}")[:].rearrange("p (h b i) -> p h b i", b=GB, i=POOL))
                for q in range(Q):
                    act.wait_ge(d1_ready, Q * g + q + 1)
                    nc.scalar.activation(e1[:], e1[:], ACT.Exp, scale=AGENT_SCALE).then_inc(e1_ready, 1)
                    act.wait_ge(d2_ready, Q * g + q + 1)
                    nc.scalar.activation(e2[:], e2[:], ACT.Exp, scale=AGENT_SCALE).then_inc(e2_ready, 1)
                    wait_full(act, g, f"p1T{q}")
                    src = ps(f"p1T{q}")[:, 0:512].rearrange("p (t h) -> p t h", h=HI)
                    cp(p1T[0:64, :, 0, :], src[0:64])
                    cp(p1T[64:128, :, 1, :], src[64:128]).then_inc(p1T_ready, 1)
                    if q == 0:
                        act.wait_ge(Kx_ready, 16 * XH * g + 16 * XH)
                    moved(f"p2T{q}", p2T[:, 512 * q:512 * q + 512], p2T_ready, ps(f"p2T{q}")[:, 0:512])
                    moved(f"PX{q}", PX[:, 8 * q:8 * q + 8, :], PX_ready,
                          ps(f"PX{q}")[:].rearrange("p (b h) -> p b h", h=HI))
                for n in range(2):
                    moved(f"UT{n}", UT[:, :, 64 * n:64 * n + 64].rearrange("p b (h i) -> p h b i", i=POOL), UT_ready,
                          ps(f"UT{n}")[:].rearrange("p (h b i) -> p h b i", b=GB, i=POOL))
                moved("xnT2", xnT[:, 0:TOK], xnT_ready)
                moved("QT", QTs[:], QT_ready)
                for t in range(T + 1):
                    if t < T:
                        act.wait_ge(dx_ready, T * g + t + 1)
                        nc.scalar.activation(pr[:, t % 2], pr[:, t % 2], ACT.Exp, scale=X_SCALE).then_inc(pr_ready, 1)
                    if t >= 1:
                        u = t - 1
                        if u >= 2:
                            wait_full(act, g, f"OL{u - 2}")
                        moved(f"PT{u}", pT[:, u % 2], pT_ready,
                              ps(f"PT{u}")[:].rearrange("p (j q) -> p j q", q=P))
                moved("xnT3", xnT[:, 0:TOK], xnT_ready)
                act.wait_ge(dg_ready, g + 1)
                nc.scalar.activation(gex, ga, ACT.Exp).then_inc(gex_ready, 1)

                def silu(c, n):
                    p = order[n]
                    name = f"H{c}_{p}"
                    wait_full(act, g, name)
                    k = (EP + 1) * c + n
                    if k >= 2:
                        act.wait_ge(hT_ready, (EP + 1) * CHUNKS * g + k - 1)
                    nc.scalar.activation(sil[:, n_of(c, n) % 2, :], ps(name)[:, 0:512], ACT.Silu,
                                         bias=b1[:, p:p + 1]).then_inc(sil_ready, 1)

                silu(0, 0)
                moved("combT", combT, combT_ready)
                moved("combS", combsT, combT_ready, ps("combS")[:, 0:512].bitcast(bf16))
                for n in range(1, EP + 1):
                    silu(0, n)
                for n in range(EP + 1):
                    silu(1, n)

        @block.vector
        def _(dve):
            V = nc.vector
            with dve.Fori(0, GROUPS) as g:
                links = [0]

                def link(ins):
                    links[0] += 1
                    ins.then_inc(vec, 1)
                    dve.wait_ge(vec, VEC_LINKS * g + links[0])

                def norm(n):
                    src = xin if n == 0 else xr
                    for t in range(T):
                        last = V.bn_stats(stats[:, t, :], src[:, t, :])
                    link(last)
                    even, odd = stats[:, :, 0:3], stats[:, :, 3:6]
                    V.tensor_tensor(mean2[:], even[:, :, 1], odd[:, :, 1], ALU.add)
                    V.tensor_tensor(diff[:], even[:, :, 1], odd[:, :, 1], ALU.subtract)
                    link(V.tensor_tensor(sqd[:], even[:, :, 2], odd[:, :, 2], ALU.add))
                    V.tensor_scalar(mean[:], mean2[:], 0.5, None, ALU.mult)
                    V.tensor_tensor(diff2[:], diff[:], diff[:], ALU.mult)
                    link(V.tensor_scalar(sqd2[:], sqd[:], 1.0 / D, EPS, ALU.mult, ALU.add))
                    V.scalar_tensor_tensor(ve[:], diff2[:], 0.25, sqd2[:], ALU.mult, ALU.add).then_inc(var_ready, 1)
                    dve.wait_ge(rstd_ready, 3 * g + n + 1)
                    if n == 0:
                        dve.wait_ge(stored, 16 * Q * g)
                    for t in range(T):
                        last = V.tensor_scalar(xn[:, t, :], src[:, t, :], mean[:, t:t + 1], rstd[:, t:t + 1],
                                               ALU.subtract, ALU.mult)
                    last.then_inc(xn_ready, 1)

                def b3d(ap, shape):
                    return ap.to_broadcast(shape)

                dve.wait_ge(x_loaded, 16 * g + 16)
                norm(0)
                dve.wait_ge(xr_ready, g + 1)
                for v in range(2):
                    wait_full(dve, g, f"V{v}")
                    for r in range(2):
                        last = V.tensor_tensor(
                            Vb[:, QT * v:QT * v + QT, :, r, :],
                            ps(f"V{v}")[:].rearrange("p (t a j c) -> p t a j c", a=2, j=XH // 2, c=16)[:, :, r],
                            parity[:].rearrange("p (j a) c -> p j (a c)", a=2).unsqueeze(1).to_broadcast(
                                [P, QT, XH // 2, 16]), ALU.mult)
                    last.then_inc(V_ready, 1)
                    if v == 0:
                        dve.wait_ge(xnT_ready, 3 * g + 1)
                        V.tensor_reduce(pooled[:], xnT[:, 0:TOK].rearrange("p (k s) -> p k s", s=S // POOL), AX,
                                        ALU.add).then_inc(pooled_ready, 1)
                for n in (1, 3):
                    wait_full(dve, g, f"M{n}")
                    V.tensor_copy(M[:, n // 2, :, 64:128].rearrange("p b (h i) -> p h b i", i=POOL),
                                  ps(f"M{n}")[:].rearrange("p (h b i) -> p h b i", b=GB, i=POOL)).then_inc(Md_ready, 1)
                for q in range(Q):
                    wait_full(dve, g, f"s1_{q}")
                    s1 = ps(f"s1_{q}")[:].rearrange("p (b s) -> p b s", s=P)[:, :, 0:S]
                    link(V.tensor_reduce(m1[:], s1, AX, ALU.max))
                    if q:
                        wait_full(dve, g, f"p1T{q - 1}")
                    V.tensor_tensor(e1[:], s1, m1[:].unsqueeze(2).to_broadcast([P, 8, S]),
                                    ALU.subtract).then_inc(d1_ready, 1)
                    wait_full(dve, g, f"s2_{q}")
                    s2 = ps(f"s2_{q}")[:, 0:512].rearrange("p (k i) -> p k i", i=POOL)
                    e2v = e2[:].rearrange("p t (h i) -> p (t h) i", i=POOL)
                    link(V.tensor_reduce(m2[:], s2, AX, ALU.max))
                    if q:
                        wait_full(dve, g, f"p2T{q - 1}")
                    V.tensor_tensor(e2v, s2, m2[:].unsqueeze(2).to_broadcast([P, QT * H, POOL]),
                                    ALU.subtract).then_inc(d2_ready, 1)
                    dve.wait_ge(e1_ready, Q * g + q + 1)
                    link(V.tensor_reduce(l1[:], e1[:], AX, ALU.add))
                    V.reciprocal(r1[:, 8 * q:8 * q + 8], l1[:])
                    dve.wait_ge(e2_ready, Q * g + q + 1)
                    link(V.tensor_reduce(l2[:], e2v, AX, ALU.add))
                    link(V.reciprocal(r2[:], l2[:]))
                    V.tensor_tensor(e2v, e2v, r2[:].unsqueeze(2).to_broadcast([P, QT * H, POOL]),
                                    ALU.mult).then_inc(p2_ready, 1)
                for q in range(Q):
                    wait_full(dve, g, f"U{q}")
                    V.tensor_tensor(U[:, 8 * q:8 * q + 8, :], ps(f"U{q}")[:].rearrange("p (b d) -> p b d", d=D),
                                    r1[:, 8 * q:8 * q + 8].unsqueeze(2).to_broadcast([P, 8, D]),
                                    ALU.mult).then_inc(U_ready, 1)

                def add_rows(name, q, dst):
                    wait_full(dve, g, name)
                    return V.tensor_tensor(dst[:, QT * q:QT * q + QT, :], xr[:, QT * q:QT * q + QT, :],
                                           ps(name)[:].rearrange("p (t d) -> p t d", d=D), ALU.add)

                for q in range(Q):
                    add_rows(f"Ya{q}", q, xr).then_inc(attn_added, 1)
                dve.wait_ge(attn_added, Q * g + Q)

                norm(1)

                def softmax_in(t):
                    wait_full(dve, g, f"S{t}")
                    sv = ps(f"S{t}")[:].rearrange("p (h s) -> p h s", s=S)
                    link(V.tensor_reduce(mx[:, t % 2], sv, AX, ALU.max))
                    if t >= 2:
                        wait_full(dve, g, f"PT{t - 2}")
                    V.tensor_tensor(pr[:, t % 2], sv, mx[:, t % 2].unsqueeze(2).to_broadcast([P, XH, S]),
                                    ALU.subtract).then_inc(dx_ready, 1)

                def normalise(t):
                    name = f"OL{t}"
                    wait_full(dve, g, name)
                    link(V.reciprocal(rl[:].rearrange("p s q -> p (s q)"), ps(name)[:, 256:512]))
                    V.tensor_tensor(On[:, t % 2].rearrange("p s q -> p (s q)"), ps(name)[:, 0:256],
                                    rl[:].rearrange("p s q -> p (s q)"), ALU.mult).then_inc(On_ready, 1)

                for t in range(T + 2):
                    if t < T:
                        softmax_in(t)
                    if t >= 2:
                        normalise(t - 2)
                    if t - 2 == QT:
                        add_rows("Yx0", 0, xr).then_inc(xattn_added, 1)
                add_rows("Yx1", 1, xr).then_inc(xattn_added, 1)
                dve.wait_ge(xattn_added, Q * g + Q)

                norm(2)
                wait_full(dve, g, "gate")
                lg = ps("gate")[:, 0:T * E].rearrange("p (t e) -> p t e", e=E)
                te = [P, T, E]
                link(V.tensor_reduce(g1[:], lg, AX, ALU.max))
                V.tensor_tensor(ga, lg, g1[:].unsqueeze(2).to_broadcast(te), ALU.subtract).then_inc(dg_ready, 1)
                dve.wait_ge(gex_ready, g + 1)
                link(V.tensor_reduce(g1[:], gex, AX, ALU.add))
                link(V.reciprocal(g2[:], g1[:]))
                link(V.tensor_tensor(orig, gex, g2[:].unsqueeze(2).to_broadcast(te), ALU.mult))
                link(V.tensor_tensor(sc, orig, gb[:].unsqueeze(1).to_broadcast(te), ALU.add))
                sg = sc.rearrange("p t (g e) -> p (t g) e", e=EG)
                V.tensor_tensor(ps6[:, :, 0:2], sg[:, :, 0:2], sg[:, :, 2:4], ALU.add)
                V.tensor_tensor(ps6[:, :, 2:4], sg[:, :, 0:3:2], sg[:, :, 1:4:2], ALU.add)
                V.tensor_tensor(ps6[:, :, 4:5], sg[:, :, 0:1], sg[:, :, 3:4], ALU.add)
                link(V.tensor_tensor(ps6[:, :, 5:6], sg[:, :, 1:2], sg[:, :, 2:3], ALU.add))
                link(V.tensor_reduce(gs[:], ps6, AX, ALU.max))
                gsv = gs[:].rearrange("p (t g) -> p t g", g=EG)
                gg = [P, T, EG, EG]
                other, own = gsv.unsqueeze(2).to_broadcast(gg), gsv.unsqueeze(3).to_broadcast(gg)
                V.tensor_tensor(gta, other, own, ALU.is_gt)
                link(V.tensor_tensor(gtb, other, own, ALU.is_equal))
                link(V.tensor_tensor(gtb, gtb, lower[:].unsqueeze(1).to_broadcast(gg), ALU.mult))
                link(V.tensor_tensor(gta, gta, gtb, ALU.add))
                link(V.tensor_reduce(rank[:], gta.rearrange("p t a b -> p (t a) b"), AX, ALU.add))
                link(V.tensor_scalar(keep[:], rank[:], 2.0, None, ALU.is_lt))
                link(V.tensor_scalar(kb[:], keep[:], FAR, -FAR, ALU.mult, ALU.add))
                tg = tv.rearrange("p t (g e) -> p (t g) e", e=EG)
                ge = [P, T * EG, EG]
                link(V.tensor_tensor(tg, sg, keep[:].unsqueeze(2).to_broadcast(ge), ALU.mult))
                link(V.tensor_tensor(tg, tg, kb[:].unsqueeze(2).to_broadcast(ge), ALU.add))
                for k in range(2):
                    link(V.tensor_reduce(g1[:], tv, AX, ALU.max))
                    link(V.tensor_tensor(oh[:, k], tv, g1[:].unsqueeze(2).to_broadcast(te), ALU.is_equal))
                    link(V.tensor_tensor(oh[:, k], oh[:, k], down[:].unsqueeze(1).to_broadcast(te), ALU.mult))
                    link(V.tensor_reduce(g2[:], oh[:, k], AX, ALU.max))
                    link(V.tensor_tensor(oh[:, k], oh[:, k], g2[:].unsqueeze(2).to_broadcast(te), ALU.is_equal))
                    if k == 0:
                        link(V.scalar_tensor_tensor(tv, oh[:, 0], -FARTHER, tv, ALU.mult, ALU.add))
                link(V.tensor_tensor(tv, oh[:, 0], oh[:, 1], ALU.add))
                cw = comb[:, :, 0:E]
                link(V.tensor_tensor(cw, tv, orig, ALU.mult))
                link(V.tensor_copy(combs[:, :, 0:E], cw))
                link(V.tensor_tensor(tv, cw, combs[:, :, 0:E], ALU.subtract))
                link(V.tensor_copy(combs[:, :, E:2 * E], tv))
                link(V.tensor_tensor(tv, tv, combs[:, :, E:2 * E], ALU.subtract))
                V.tensor_copy(combs[:, :, 2 * E:3 * E], tv).then_inc(comb_ready, 1)

                def hidden(c, n):
                    p = order[n]
                    k = n_of(c, n)
                    name = f"H{c}_{p}"
                    wait_full(dve, g, name)
                    dve.wait_ge(sil_ready, (EP + 1) * CHUNKS * g + k + 1)
                    shared = p == EP
                    if shared:
                        if c:
                            wait_full(dve, g, "Ym0")
                        V.scalar_tensor_tensor(hT[:, n % 2, :], ps(name)[:, 512:1024], b3[:, p:p + 1],
                                               sil[:, k % 2, :], ALU.add, ALU.mult).then_inc(hT_ready, 1)
                        return
                    V.scalar_tensor_tensor(hid[:, n % 2, :], ps(name)[:, 512:1024], b3[:, p:p + 1],
                                           sil[:, k % 2, :], ALU.add, ALU.mult).then_inc(hid_ready, 1)
                    dve.wait_ge(hid_ready, EP * (CHUNKS * g + c) + p + 1)
                    wait_full(dve, g, f"C{c}_{p}")
                    V.tensor_tensor(hT[:, n % 2, :], hid[:, n % 2, :], ps(f"C{c}_{p}")[:], ALU.mult).then_inc(hT_ready, 1)

                for c in range(CHUNKS):
                    for n in range(EP + 1):
                        hidden(c, n)
                    add_rows(f"Ym{c}", c, xo).then_inc(out_ready, 1)
                assert links[0] == VEC_LINKS, links[0]


_INS = ['x', 'ctx_1024', 'L0_attn_Wqkv', 'L0_attn_Wo', 'L0_attn_bo', 'L0_xattn_Wq', 'L0_xattn_Wk', 'L0_xattn_Wv',
        'L0_xattn_Wo', 'L0_ffn_gate_w', 'L0_ffn_gate_b', 'L0_ffn_We1', 'L0_ffn_be1', 'L0_ffn_We2', 'L0_ffn_be2',
        'L0_ffn_We3', 'L0_ffn_be3', 'L0_ffn_ws1', 'L0_ffn_bs1', 'L0_ffn_ws2', 'L0_ffn_bs2', 'L0_ffn_ws3', 'L0_ffn_bs3']


def kernel(**inputs):
    import concourse.bacc as bacc
    from concourse.bass_utils import run_bass_kernel_spmd

    nc = bacc.Bacc("TRN2", target_bir_lowering=False, num_devices=1)
    arrays, args = {}, []
    for name in _INS:
        a = np.ascontiguousarray(inputs[name])
        arrays[f"in_{name}"] = a
        args.append(nc.dram_tensor(f"in_{name}", a.shape, mybir.dt.from_np(a.dtype), kind="ExternalInput").ap())
    out = nc.dram_tensor("out_x", arrays["in_x"].shape, mybir.dt.float32, kind="ExternalOutput").ap()
    decoder_block(nc, *args, out)
    r = run_bass_kernel_spmd(nc, [arrays], core_ids=[0])
    return r.results[0]["out_x"]
```

```python
import numpy as np
import concourse.bass as bass
from concourse import mybir
from contextlib import ExitStack


def decoder_block(nc, x, ctx_in, Wqkv, Wo_a, bo, Wq, Wk, Wv, Wo_x, gate_w, gate_b,
                  We1, be1, We2, be2, We3, be3, ws1, bs1, ws2, bs2, ws3, bs3, out):
    fp32, bf16 = mybir.dt.float32, mybir.dt.bfloat16
    ALU, ACT, AX = mybir.AluOpType, mybir.ActivationFunctionType, mybir.AxisListType.X

    B, S, D = x.shape
    P = 128
    GB = 16
    GROUPS = B // GB
    TOK = GB * S
    T = TOK // P
    QT = 4
    Q = T // QT
    H, POOL, DH = 16, 8, 64
    HI = H * POOL
    XH, XC = 16, 8
    HALF = XH // 2
    E, EG, EI = 16, 4, 64
    EP = E // 2
    CH = 512
    CHUNKS = TOK // CH
    EPS = 1e-5
    AGENT_SCALE = DH ** -0.5 / (S // POOL)
    X_SCALE = XC ** -0.5
    MASKED = -1e9 / X_SCALE
    FAR, FARTHER = 1e30, 1e32

    x_v = x.rearrange("(g b) s d -> g (b s) d", b=GB).rearrange("g (t p) d -> g p t d", p=P)
    c_v = ctx_in.rearrange("(g b) s d -> g (b s) d", b=GB).rearrange("g (t p) d -> g p t d", p=P)
    o_v = out.rearrange("(g b) s d -> g (b s) d", b=GB).rearrange("g (t p) d -> g p t d", p=P)

    att = ["ctxT_0", "ctxT_1", "KT_0", "KT_1"] + [f"V_{n}" for n in range(4)] + ["xnT1_0", "xnT1_1"]
    att += [f"M_{n}" for n in range(8)] + ["s1_0", "s1_1", "s2_0", "s1_2", "s1_3", "s2_1"]
    att += ["p1T_0", "p2T_0", "PX_0", "PX_1", "p1T_1", "p2T_1", "PX_2", "PX_3"]
    att += [f"UT_{n}" for n in range(4)] + [f"U_{n}" for n in range(4)] + ["Ya_0", "Ya_1"]
    att += ["xnT2_0", "xnT2_1", "QT_0", "QT_1"] + [f"S_{n}" for n in range(2 * T)]
    UNITS = CHUNKS * (EP + 1)
    PAIRED = [k for k in range(UNITS) if k % (EP + 1)]
    pair = [k % (EP + 1) - 1 if k % (EP + 1) else EP for k in range(UNITS)]
    RINGS = {"att": (att, 4),
             "h1": (["xnT3_0"] + [f"H1_{k}" for k in range(UNITS)], 1),
             "h3": (["xnT3_1"] + [f"H3_{k}" for k in range(UNITS)], 1),
             "c": (["gate", "combT_0", "combT_1", "combS"] + [f"C_{k}" for k in PAIRED], 1),
             "y": (["Y_0", "Y_1"], 1),
             "pt": ([f"PT_{n}" for n in range(2 * T)], 2),
             "ol": ([f"OL_{t}" for t in range(T)], 1),
             "yx": ([f"Yx_{t}" for t in range(T)], 1)}
    place = {}
    for ring, (names, n) in RINGS.items():
        for at, name in enumerate(names):
            k = at % n
            place[name] = (ring, k, at // n, len(range(k, len(names), n)), at)

    with ExitStack() as ctx:
        def sb(name, shape, dt=fp32):
            return ctx.enter_context(nc.sbuf_tensor(name, shape, dt))

        def sem(name):
            return ctx.enter_context(nc.semaphore(name))

        KQ = sb("KQ", [P, 8, TOK])
        Kx, Qx = KQ[:, 0:4, :], KQ[:, 4:8, :]
        wqkv = KQ[:, 0:3, :].rearrange("p a n -> p (a n)")
        wT = KQ[:, 3:6, :].rearrange("p a (b n) -> p (a b) n", n=P)
        woa = KQ[:, 6:7, :].rearrange("p a (b n) -> p (a b) n", n=D)
        xw = KQ[:, 7, 0:512].rearrange("p (a n) -> p a n", n=D)
        gw = KQ[0:E, 7, 512:512 + D]
        A1 = sb("A1", [P, H, D])
        A2 = sb("A2", [P, H, D])
        Wvo = sb("Wvo", [P, H, D])
        xwT = sb("xwT", [P, 4, D])
        woM = sb("woM", [P, 2, 2, D])
        w1 = sb("w1", [P, E + 2, EI])
        w3 = sb("w3", [P, E + 2, EI])
        w2 = sb("w2", [P, EP + 1, D])
        b1 = sb("b1", [P, EP + 1])
        b3 = sb("b3", [P, EP + 1])
        b2x = sb("b2x", [P, D])
        gwT = sb("gwT", [P, E])
        gb = sb("gb", [P, E])
        bo_b = sb("bo_b", [P, D])
        ident = sb("ident", [P, P])
        identb = sb("identb", [P, P], bf16)
        maskb = sb("maskb", [P, HALF, S], bf16)
        bones = sb("bones", [P, 2, 2, XC])
        planes = sb("planes", [P, 4, 4])
        plane = sb("plane", [P, 4])
        onehot3 = sb("onehot3", [P, E], bf16)
        spread = sb("spread", [P, EP, 2, EI], bf16)
        lower = sb("lower", [P, EG, EG])
        down = sb("down", [P, E])
        mhalf = sb("mhalf", [P, T])
        xin = sb("xin", [P, T, D])
        cin = sb("cin", [P, T, D])
        xr = sb("xr", [P, T, D])
        xe = sb("xe", [P, T, D])
        xn = sb("xn", [P, T, D])
        xn3 = sb("xn3", [P, T, D])
        xo = xn3
        xnT = sb("xnT", [P, TOK + S])
        xnT3 = sb("xnT3", [P, TOK])
        stats = sb("stats", [P, T, 6])
        mean, mean2, diff, diff2, sqd, sqd2, ve, rstd = [sb(f"norm{k}", [P, T]) for k in range(8)]
        pooled = sb("pooled", [P, GB * POOL])
        M = sb("M", [P, 2, GB, HI])
        e1 = sb("e1", [P, Q, 8, S])
        m1 = sb("m1", [P, 4, 4])
        l1 = sb("l1", [P, 8])
        r1 = sb("r1", [P, GB])
        e2 = sb("e2", [P, Q, QT, HI])
        m2 = sb("m2", [P, QT * H])
        l2 = sb("l2", [P, QT * H])
        r2 = sb("r2", [P, QT * H])
        p1T = sb("p1T", [P, QT, 2, HI])
        p2T = sb("p2T", [P, TOK])
        PX = sb("PX", [P, GB, HI])
        UT = sb("UT", [P, GB, HI])
        U = PX
        ctxT = sb("ctxT", [P, TOK])
        Vb = sb("Vb", [P, T, XH // 2, 2, 2 * XC])
        mx = sb("mx", [P, 2, HALF])
        pr = M[:, 0].rearrange("p b h -> p (b h)").rearrange("p (k h s) -> p k h s", k=4, s=S)
        pT = M[:, 1].rearrange("p b h -> p (b h)").rearrange("p (k j q) -> p k j q", k=4, q=P)
        rl = sb("rl", [P, 2 * P])
        On = sb("On", [P, 2, 2, P])
        TE = T * E
        g1 = sb("g1", [P, T])
        g2 = sb("g2", [P, T])
        g3 = sb("g3", [P, T])
        gs = sb("gs", [P, T * EG])
        rank = sb("rank", [P, T * EG])
        keep = sb("keep", [P, T * EG])
        kb = sb("kb", [P, T * EG])
        ga, gex, orig, sc, tv = [sb(f"gate{k}", [P, T, E]) for k in range(5)]
        gta, gtb = [sb(f"beats{k}", [P, T, EG, EG]) for k in range(2)]
        ps6 = sb("ps6", [P, T * EG, 6])
        oh = sb("oh", [P, 2, T, E])
        comb = sb("comb", [P, T, P])
        combs = sb("combs", [P, T, P], bf16)
        combT = sb("combT", [P, TOK])
        combsT = sb("combsT", [P, TOK], bf16)
        sil = sb("sil", [P, 2, CH])
        hid = sb("hid", [P, 2, CH])
        hT = sb("hT", [P, 2, CH])

        two = [ctx.enter_context(nc.psum_tensor(f"banks{k}", [P, 1024], fp32)) for k in range(4)]
        banks = [two[k // 2][:, 512 * (k % 2):512 * (k % 2) + 512] for k in range(8)]
        bank = {"att": banks[0:4], "h1": banks[4:5], "h3": banks[5:6], "c": banks[6:7], "y": banks[7:8],
                "pt": banks[4:6], "ol": banks[6:7], "yx": banks[7:8]}

        full = {(r, k): sem(f"{r}{k}_full") for r, (_, n) in RINGS.items() for k in range(n)}

        loaded_w, loaded_m, spread_wo = sem("loaded_w"), sem("loaded_m"), sem("spread_wo")
        const_step, consts, plane_ready = sem("const_step"), sem("consts"), sem("plane_ready")
        setup_ps, setup_cp = sem("setup_ps"), sem("setup_cp")
        x_loaded, c_loaded, xr_ready = sem("x_loaded"), sem("c_loaded"), sem("xr_ready")
        var_ready, rstd_ready, xn_ready, xnT_ready = (
            sem("var_ready"), sem("rstd_ready"), sem("xn_ready"), sem("xnT_ready"))
        var3_ready, rstd3_ready, xn3_ready, xnT3_ready = (
            sem("var3_ready"), sem("rstd3_ready"), sem("xn3_ready"), sem("xnT3_ready"))
        ctxT_ready, Kx_ready, V_ready = sem("ctxT_ready"), sem("Kx_ready"), sem("V_ready")
        pooled_ready, M_ready = sem("pooled_ready"), sem("M_ready")
        d1_ready, d2_ready, e1_ready, e2_ready = sem("d1_ready"), sem("d2_ready"), sem("e1_ready"), sem("e2_ready")
        p2_ready, p1T_ready, p2T_ready = sem("p2_ready"), sem("p1T_ready"), sem("p2T_ready")
        PX_ready, UT_ready, U_ready, attn_added = sem("PX_ready"), sem("UT_ready"), sem("U_ready"), sem("attn_added")
        Qx_ready, dx_ready, pr_ready, pT_ready = sem("Qx_ready"), sem("dx_ready"), sem("pr_ready"), sem("pT_ready")
        On_ready, xattn_added = sem("On_ready"), sem("xattn_added")
        dg_ready, gex_ready, comb_ready, combT_ready = (
            sem("dg_ready"), sem("gex_ready"), sem("comb_ready"), sem("combT_ready"))
        sil_ready, hid_ready, hT_ready = sem("sil_ready"), sem("hid_ready"), sem("hT_ready")
        out_ready, stored = sem("out_ready"), sem("stored")
        vec_a, vec_e = sem("vec_a"), sem("vec_e")
        LINKS_A, LINKS_E = 43, 36

        read = {"gate": (dg_ready, 1, 0), "combT_0": (combT_ready, 3, 0), "combT_1": (combT_ready, 3, 1),
                "combS": (combT_ready, 3, 2)}
        for n in range(2):
            read |= {f"xnT1_{n}": (xnT_ready, 4, n), f"xnT2_{n}": (xnT_ready, 4, 2 + n),
                     f"xnT3_{n}": (xnT3_ready, 2, n), f"ctxT_{n}": (ctxT_ready, 2, n), f"KT_{n}": (Kx_ready, 2, n),
                     f"QT_{n}": (Qx_ready, 2, n), f"Y_{n}": (out_ready, 2, n), f"s2_{n}": (d2_ready, 2, n),
                     f"p1T_{n}": (p1T_ready, 2, n), f"p2T_{n}": (p2T_ready, 2, n), f"Ya_{n}": (attn_added, 2, n)}
        for n in range(4):
            read |= {f"V_{n}": (V_ready, 4, n), f"s1_{n}": (d1_ready, 4, n), f"PX_{n}": (PX_ready, 4, n),
                     f"UT_{n}": (UT_ready, 4, n), f"U_{n}": (U_ready, 4, n)}
        for n in range(8):
            read |= {f"M_{n}": (M_ready, 8, n)}
        for n in range(2 * T):
            read |= {f"S_{n}": (dx_ready, 2 * T, n), f"PT_{n}": (pT_ready, 2 * T, n)}
        for t in range(T):
            read |= {f"OL_{t}": (On_ready, T, t), f"Yx_{t}": (xattn_added, T, t)}
        for k in range(UNITS):
            read[f"H1_{k}"] = (sil_ready, UNITS, k)
            if k in PAIRED:
                read |= {f"H3_{k}": (hid_ready, len(PAIRED), PAIRED.index(k)), f"C_{k}": (hT_ready, UNITS, k)}
            else:
                read[f"H3_{k}"] = (hT_ready, UNITS, k)

        block = ctx.enter_context(nc.Block())

        def ps(name):
            return bank[place[name][0]][place[name][1]]

        def wait_free(pe, g, name):
            ring, k, use, _, at = place[name]
            if use:
                signal, per, n = read[RINGS[ring][0][at - RINGS[ring][1]]]
                pe.wait_ge(signal, g * per + n + 1)
            elif ring == "yx":
                pe.wait_ge(out_ready, CHUNKS * g)

        def wait_full(eng, g, name):
            ring, k, use, per, _ = place[name]
            eng.wait_ge(full[ring, k], g * per + use + 1)

        def fulled(name):
            return full[place[name][:2]]

        def run(eng, both):
            both(None, 0)
            with eng.Fori(0, GROUPS - 1) as e:
                both(e, e + 1)
            both(GROUPS - 1, None)

        SETUP = [("T", s) for s in range(3)] + [("W", s) for s in range(6)] + [("X", 0)]

        @block.sync
        def _(sp):
            sp.dma_start(wqkv, Wqkv).then_inc(loaded_w, 16)
            sp.dma_start(woa, Wo_a.rearrange("(b p) d -> p b d", p=P)).then_inc(loaded_w, 16)
            for n, w in enumerate((Wq, Wk, Wv, Wo_x)):
                sp.dma_start(xw[:, n, :], w).then_inc(loaded_w, 16)
            sp.dma_start(gw, gate_w).then_inc(loaded_w, 16)
            sp.dma_start(xin[:], x_v[0]).then_inc(x_loaded, 16)
            sp.dma_start(cin[:], c_v[0]).then_inc(c_loaded, 16)
            sp.dma_start(gb[:], gate_b.partition_broadcast(P)).then_inc(loaded_m, 16)
            sp.dma_start(bo_b[:], bo.partition_broadcast(P)).then_inc(loaded_m, 16)
            for w_sb, we, ws in ((w1, We1, ws1), (w3, We3, ws3)):
                sp.dma_start(w_sb[:, 0:E, :], we.rearrange("e d i -> d e i")).then_inc(loaded_m, 16)
                sp.dma_start(w_sb[:, E:E + 2, :], ws.rearrange("d (e i) -> d e i", i=EI)).then_inc(loaded_m, 16)
            sp.dma_start(w2[:, 0:EP, :], We2.rearrange("(p a) i d -> (a i) p d", a=2)).then_inc(loaded_m, 16)
            sp.dma_start(w2[:, EP, :], ws2).then_inc(loaded_m, 16)
            with nc.allow_non_contiguous_dma("biases, a column each, once"):
                for b_sb, be, bs in ((b1, be1, bs1), (b3, be3, bs3)):
                    sp.dma_start(b_sb[:, 0:EP], be.rearrange("(p a) i -> (a i) p", a=2)).then_inc(loaded_m, 16)
                    sp.dma_start(b_sb[:, EP:EP + 1], bs.rearrange("(p a) -> p a", a=1)).then_inc(loaded_m, 16)
            sp.wait_ge(consts, 1)
            sp.dma_start(b2x[0:E, :], be2).then_inc(loaded_m, 16)
            sp.dma_start(b2x[E:E + 1, :], bs2.rearrange("(a d) -> a d", a=1)).then_inc(loaded_m, 16)
            sp.wait_ge(consts, 3)
            sp.wait_ge(setup_cp, len(SETUP))
            for s in range(2):
                for b in range(2):
                    for gq in range(4):
                        sp.dma_start(woM[32 * gq + 16 * b:32 * gq + 16 * b + 16, s, b, :],
                                     xwT[64 * s + 16 * gq:64 * s + 16 * gq + 16, 3, :]).then_inc(spread_wo, 16)
            with sp.Fori(1, GROUPS) as g:
                sp.wait_ge(xr_ready, g)
                sp.dma_start(xin[:], x_v[bass.ds(g, 1)].rearrange("a p t d -> (a p) t d")).then_inc(x_loaded, 16)
                sp.wait_ge(ctxT_ready, 2 * g)
                sp.dma_start(cin[:], c_v[bass.ds(g, 1)].rearrange("a p t d -> (a p) t d")).then_inc(c_loaded, 16)

        @block.gpsimd
        def _(pool):
            steps = [0]

            def step(ins):
                steps[0] += 1
                ins.then_inc(const_step, 1)
                pool.wait_ge(const_step, steps[0])

            step(nc.gpsimd.memset(b2x[:], 0.0))
            nc.gpsimd.memset(mhalf[:], -0.5).then_inc(consts, 1)
            nc.gpsimd.memset(ident[:], 0.0)
            nc.gpsimd.memset(onehot3[:], 0.0)
            nc.gpsimd.memset(maskb[:], 0.0)
            nc.gpsimd.memset(lower[:], 1.0)
            nc.gpsimd.memset(planes[:], 1.0)
            step(nc.gpsimd.memset(bones[:], 0.0))
            step(nc.gpsimd.affine_select(out=ident[:], in_=ident[:], compare_op=ALU.not_equal, fill=1.0, base=0,
                                         pattern=[[-1, P]], channel_multiplier=1))
            nc.gpsimd.tensor_copy(identb[:], ident[:]).then_inc(consts, 1)
            nc.gpsimd.memset(woM[:], 0.0)
            nc.gpsimd.memset(p1T[:], 0.0)
            nc.gpsimd.memset(Vb[:], 0.0)
            nc.gpsimd.memset(xnT[:, TOK:TOK + S], 0.0)
            nc.gpsimd.memset(combs[:], 0.0)
            step(nc.gpsimd.memset(comb[:], 0.0))
            nc.gpsimd.memset(comb[:, :, E:E + 1], 1.0)
            nc.gpsimd.iota(down[:], pattern=[[-1, E]], base=E, channel_multiplier=0,
                           allow_small_or_imprecise_dtypes=True)
            for k in range(3):
                step(nc.gpsimd.affine_select(out=onehot3[:], in_=onehot3[:], compare_op=ALU.not_equal, fill=1.0,
                                             base=-E * k, pattern=[[-1, E]], channel_multiplier=1))
            step(nc.gpsimd.affine_select(out=lower[:], in_=lower[:], compare_op=ALU.is_gt, fill=0.0, base=0,
                                         pattern=[[1, EG], [-1, EG]], channel_multiplier=0))
            step(nc.gpsimd.affine_select(out=planes[:], in_=planes[:], compare_op=ALU.is_ge, fill=0.0, base=0,
                                         pattern=[[-XC, 4], [-4 * XC, 4]], channel_multiplier=1))
            step(nc.gpsimd.affine_select(out=planes[:], in_=planes[:], compare_op=ALU.is_ge, fill=0.0, base=XC - 1,
                                         pattern=[[XC, 4], [4 * XC, 4]], channel_multiplier=-1))
            for r in range(2):
                rr = slice(64 * r, 64 * r + 64)
                step(nc.gpsimd.affine_select(out=maskb[rr], in_=maskb[rr], compare_op=ALU.is_ge, fill=MASKED, base=0,
                                             pattern=[[0, HALF], [-1, S]], channel_multiplier=1))
                step(nc.gpsimd.memset(bones[rr, :, r, :], 1.0))
            step(nc.gpsimd.tensor_copy(spread[:].rearrange("r p a i -> r (p a) i"),
                                       onehot3[:].unsqueeze(2).to_broadcast([P, E, EI])))
            nc.gpsimd.memset(mhalf[:], -0.5).then_inc(consts, 1)
            pool.wait_ge(consts, 3)
            pool.wait_ge(setup_cp, len(SETUP))
            nc.gpsimd.memset(Qx, 0.0).then_inc(consts, 1)
            pool.wait_ge(loaded_m, 16 * 14)

            def store(e, c):
                pool.wait_ge(out_ready, CHUNKS * e + c + 1)
                dst = o_v[e] if isinstance(e, int) else o_v[bass.ds(e, 1)].rearrange("a p t d -> (a p) t d")
                pool.dma_start(dst[:, QT * c:QT * c + QT, :], xo[:, QT * c:QT * c + QT, :]).then_inc(stored, 16)

            def both(e, g):
                if e is not None:
                    pool.wait_ge(var3_ready, e + 1)
                    nc.gpsimd.tensor_tensor(rstd[:], ve[:], mhalf[:], ALU.pow).then_inc(rstd3_ready, 1)
                if g is not None:
                    pool.wait_ge(var_ready, 2 * g + 1)
                    nc.gpsimd.tensor_tensor(rstd[:], ve[:], mhalf[:], ALU.pow).then_inc(rstd_ready, 1)
                    pool.wait_ge(xn_ready, 2 * g + 1)
                    if e is not None:
                        pool.wait_ge(xattn_added, T * g)
                    nc.gpsimd.tensor_tensor(xr[:], xin[:], bo_b[:].unsqueeze(1).to_broadcast([P, T, D]),
                                            ALU.add).then_inc(xr_ready, 1)
                if e is not None:
                    store(e, 0)
                if g is not None:
                    pool.wait_ge(var_ready, 2 * g + 2)
                    nc.gpsimd.tensor_tensor(rstd[:], ve[:], mhalf[:], ALU.pow).then_inc(rstd_ready, 1)
                if e is not None:
                    store(e, 1)

            run(pool, both)
            pool.wait_ge(stored, 16 * CHUNKS * GROUPS)

        @block.tensor
        def _(pe):
            mm, turn_over = nc.tensor.matmul, nc.tensor.transpose
            pe.wait_ge(consts, 2)
            pe.wait_ge(loaded_w, 16 * 7)
            for n, (kind, s) in enumerate(SETUP):
                dst = two[n % 3]
                if n >= 3:
                    pe.wait_ge(setup_cp, n - 2)
                if kind == "T":
                    for k in range(8):
                        c0 = (8 * s + k) * P
                        last = turn_over(dst[:, P * k:P * k + P], wqkv[:, c0:c0 + P], ident[:])
                elif kind == "W":
                    if s == 0:
                        pe.wait_ge(setup_cp, 3)
                    for k in range(8):
                        h = 8 * (s % 2) + k
                        rr = slice(64 * (h % 2), 64 * (h % 2) + 64)
                        a = (wT[rr, h // 2, :], wT[rr, h // 2, :], wT[rr, 16 + h // 2, :])[s // 2]
                        b = (wT[rr, 8 + h // 2, :], wT[rr, h // 2, :], woa[rr, h // 2, :])[s // 2]
                        c0 = 512 * (h % 2) + P * (k // 2)
                        last = mm(dst[:, c0:c0 + P], a, b, start=True, stop=True)
                else:
                    for k in range(4):
                        turn_over(dst[:, P * k:P * k + P], xw[:, k, :], ident[:])
                    last = turn_over(dst[:, 512:512 + E], gw, ident[0:E, 0:E])
                last.then_inc(setup_ps, 1)
            pe.wait_ge(setup_cp, len(SETUP))
            pe.wait_ge(spread_wo, 16 * 16)
            pe.wait_ge(loaded_m, 16 * 14)
            pe.wait_ge(consts, 4)

            def four(g, name, src, n):
                wait_free(pe, g, name)
                for t in range(4):
                    last = turn_over(ps(name)[:, P * t:P * t + P], src[:, 4 * n + t, :], ident[:])
                last.then_inc(fulled(name), 1)

            def up(e, k):
                for ring, w in (("H1", w1), ("H3", w3)):
                    name = f"{ring}_{k}"
                    wait_free(pe, e, name)
                    mm(ps(name)[:], w[:, 2 * pair[k]:2 * pair[k] + 2, :],
                       xnT3[:, CH * (k // (EP + 1)):CH * (k // (EP + 1)) + CH], start=True,
                       stop=True).then_inc(fulled(name), 1)

            def weight(e, k):
                name = f"C_{k}"
                c = k // (EP + 1)
                wait_free(pe, e, name)
                mm(ps(name)[:], spread[:, pair[k], :, :], combsT[:, CH * c:CH * c + CH], start=True,
                   stop=True).then_inc(fulled(name), 1)

            def down_to(e, k):
                c, n = k // (EP + 1), k % (EP + 1)
                name = f"Y_{c}"
                if n == 0:
                    wait_free(pe, e, name)
                pe.wait_ge(hT_ready, UNITS * e + k + 1)
                for t in range(4):
                    mm(ps(name)[:, P * t:P * t + P], hT[:, k % 2, P * t:P * t + P], w2[:, pair[k], :],
                       start=(n == 0 and t == 0), stop=False, skip_group_check=True)
                if n == EP:
                    for t in range(4):
                        t0 = CH * c + P * t
                        last = mm(ps(name)[:, P * t:P * t + P], combT[:, t0:t0 + P], b2x[:],
                                  start=False, stop=True, skip_group_check=True)
                    last.then_inc(fulled(name), 1)

            def unit(e, k):
                if e is None:
                    return
                up(e, k)
                if k in PAIRED:
                    weight(e, k)
                if k:
                    down_to(e, k - 1)

            def scores_1(g, n):
                name = f"s1_{n}"
                wait_free(pe, g, name)
                if n == 0:
                    pe.wait_ge(M_ready, 8 * g + 4)
                for k in range(4):
                    b = 4 * n + k
                    last = mm(ps(name)[:, P * k:P * k + P], M[:, 0, b, :], xnT[:, S * b:S * b + P],
                              start=True, stop=True)
                last.then_inc(fulled(name), 1)

            def scores_2(g, q):
                name = f"s2_{q}"
                wait_free(pe, g, name)
                if q == 0:
                    pe.wait_ge(M_ready, 8 * g + 8)
                for k in range(8):
                    b, r = 8 * q + k, k % 2
                    last = mm(ps(name)[64 * r:64 * r + 64, P * (k // 2):P * (k // 2) + P],
                              xnT[:, S * b:S * b + S], M[:, 1, b, :], start=True, stop=True)
                last.then_inc(fulled(name), 1)

            def turn_probs(g, q):
                name = f"p1T_{q}"
                wait_free(pe, g, name)
                pe.wait_ge(e1_ready, 2 * g + q + 1)
                for t in range(4):
                    last = turn_over(ps(name)[:, P * t:P * t + P],
                                     e1[:, q, 2 * t:2 * t + 2, :].rearrange("p b s -> p (b s)"), ident[:])
                last.then_inc(fulled(name), 1)
                name = f"p2T_{q}"
                wait_free(pe, g, name)
                pe.wait_ge(p2_ready, 2 * g + q + 1)
                for t in range(4):
                    last = turn_over(ps(name)[:, P * t:P * t + P], e2[:, q, t, :], ident[:])
                last.then_inc(fulled(name), 1)

            def pool_tokens(g, q):
                pe.wait_ge(p1T_ready, 2 * g + q + 1)
                for k in range(2):
                    name = f"PX_{2 * q + k}"
                    wait_free(pe, g, name)
                    for t in range(2):
                        last = mm(ps(name)[:, 256 * t:256 * t + 256], xn[:, 4 * q + 2 * k + t, :],
                                  p1T[:, 2 * k + t, :, :], start=True, stop=True)
                    last.then_inc(fulled(name), 1)

            def scores(g, t):
                for hh in range(2):
                    name = f"S_{2 * t + hh}"
                    wait_free(pe, g, name)
                    mm(ps(name)[:], identb[:], maskb[:].rearrange("p h s -> p (h s)"), start=True, stop=False,
                       skip_group_check=True)
                    for q in range(2):
                        for r in range(2):
                            b = 2 * t + r
                            last = mm(ps(name)[64 * r:64 * r + 64, 256 * q:256 * q + 256],
                                      Qx[:, 2 * hh + q, S * b:S * b + S], Kx[:, :, S * b:S * b + S],
                                      start=False, stop=True, skip_group_check=True)
                    last.then_inc(fulled(name), 1)

            def turn(g, t):
                for hh in range(2):
                    k = 2 * t + hh
                    name = f"PT_{k}"
                    wait_free(pe, g, name)
                    pe.wait_ge(pr_ready, 2 * T * g + k + 1)
                    src = pr[:, k % 4, :, :].rearrange("p h s -> p (h s)")
                    for j in range(4):
                        last = turn_over(ps(name)[:, P * j:P * j + P], src[:, P * j:P * j + P], ident[:])
                    last.then_inc(fulled(name), 1)

            def values(g, t):
                name = f"OL_{t}"
                wait_free(pe, g, name)
                for s in range(2):
                    pe.wait_ge(pT_ready, 2 * T * g + 2 * t + s + 1)
                    for gq in range(4):
                        j = 4 * s + gq
                        rr = slice(32 * gq, 32 * gq + 32)
                        p = pT[:, (2 * t + s) % 4, gq, :]
                        mm(ps(name)[rr, P * s:P * s + P], Vb[:, t, j, :, :].rearrange("p a c -> p (a c)"),
                           p, start=True, stop=True, tile_position=(0, 32 * gq))
                        last = mm(ps(name)[rr, 256 + P * s:256 + P * s + P], bones[:].rearrange("p a b c -> p (a b c)"),
                                  p, start=True, stop=True, tile_position=(0, 32 * gq))
                last.then_inc(fulled(name), 1)

            def project(g, t):
                name = f"Yx_{t}"
                wait_free(pe, g, name)
                pe.wait_ge(On_ready, T * g + t + 1)
                for s in range(2):
                    for r in range(2):
                        last = mm(ps(name)[64 * r:64 * r + 64, 0:P], On[:, t % 2, s, 64 * r:64 * r + 64],
                                  woM[:, s, r, :], start=(s == 0), stop=(s == 1))
                last.then_inc(fulled(name), 1)

            def values_of(g, n):
                wait_free_unless(g, f"V_{n}", "ctxT")
                for k in range(4):
                    b = 4 * n + k
                    for r in range(2):
                        last = mm(ps(f"V_{n}")[64 * r:64 * r + 64, P * k:P * k + P],
                                  ctxT[:, S * b:S * b + S], xwT[:, 2, :], start=True, stop=True)
                last.then_inc(fulled(f"V_{n}"), 1)

            def both(e, g):
                if g is not None:
                    pe.wait_ge(c_loaded, 16 * g + 16)
                    four(g, "ctxT_0", cin, 0)
                    four(g, "ctxT_1", cin, 1)
                if e is not None:
                    project(e, T - 1)
                if g is not None:
                    for c in range(2):
                        wait_free(pe, g, f"KT_{c}")
                        pe.wait_ge(ctxT_ready, 2 * g + c + 1)
                        mm(ps(f"KT_{c}")[:], xwT[:, 1, :], ctxT[:, 512 * c:512 * c + 512], start=True,
                           stop=True).then_inc(fulled(f"KT_{c}"), 1)
                    values_of(g, 0)
                    values_of(g, 1)
                    values_of(g, 2)
                if e is not None:
                    pe.wait_ge(xn3_ready, e + 1)
                    four(e, "xnT3_0", xn3, 0)
                    four(e, "xnT3_1", xn3, 1)
                if g is not None:
                    values_of(g, 3)
                if e is not None:
                    pe.wait_ge(xnT3_ready, 2 * e + 2)
                    for t in range(T):
                        last = mm(ps("gate")[:, E * t:E * t + E], xnT3[:, P * t:P * t + P], gwT[:],
                                  start=True, stop=True)
                    last.then_inc(fulled("gate"), 1)
                if g is not None:
                    pe.wait_ge(xn_ready, 2 * g + 1)
                    four(g, "xnT1_0", xn, 0)
                    four(g, "xnT1_1", xn, 1)
                unit(e, 0)
                if g is not None:
                    pe.wait_ge(pooled_ready, g + 1)
                    for n in range(8):
                        A = A1 if n < 4 else A2
                        wait_free_unless(g, f"M_{n}", "xnT1")
                        for k in range(4):
                            last = mm(ps(f"M_{n}")[:, P * k:P * k + P], A[:, 4 * (n % 4) + k, :], pooled[:],
                                      start=True, stop=True)
                        last.then_inc(fulled(f"M_{n}"), 1)
                if g is not None:
                    scores_1(g, 0)
                    scores_1(g, 1)
                    scores_2(g, 0)
                if e is not None:
                    pe.wait_ge(comb_ready, e + 1)
                    four(e, "combT_0", comb, 0)
                    four(e, "combT_1", comb, 1)
                    wait_free(pe, e, "combS")
                    for t in range(T):
                        last = turn_over(ps("combS")[:].bitcast(bf16)[:, P * t:P * t + P], combs[:, t, :], identb[:])
                    last.then_inc(fulled("combS"), 1)
                    pe.wait_ge(combT_ready, 3 * e + 3)
                for k in range(1, 4):
                    unit(e, k)
                if g is not None:
                    scores_1(g, 2)
                    scores_1(g, 3)
                    scores_2(g, 1)
                    unit(e, 4)
                    unit(e, 5)
                    turn_probs(g, 0)
                    unit(e, 6)
                    pool_tokens(g, 0)
                    turn_probs(g, 1)
                    unit(e, 7)
                    pool_tokens(g, 1)
                    unit(e, 8)
                    pe.wait_ge(PX_ready, 4 * g + 4)
                    for n in range(4):
                        wait_free_unless(g, f"UT_{n}", "PX")
                        for k in range(4):
                            h = 4 * n + k
                            last = mm(ps(f"UT_{n}")[:, P * k:P * k + P], Wvo[:, h, :],
                                      PX[:, :, POOL * h:POOL * h + POOL], start=True, stop=True)
                        last.then_inc(fulled(f"UT_{n}"), 1)
                    unit(e, 9)
                    pe.wait_ge(UT_ready, 4 * g + 4)
                    for n in range(4):
                        wait_free_unless(g, f"U_{n}", "UT")
                        for k in range(4):
                            last = turn_over(ps(f"U_{n}")[:, P * k:P * k + P], UT[:, 4 * n + k, :], ident[:])
                        last.then_inc(fulled(f"U_{n}"), 1)
                    unit(e, 10)
                    pe.wait_ge(p2T_ready, 2 * g + 2)
                    pe.wait_ge(U_ready, 4 * g + 4)
                    for q in range(Q):
                        wait_free_unless(g, f"Ya_{q}", "U")
                        for k in range(8):
                            b, r = 8 * q + k, k % 2
                            last = mm(ps(f"Ya_{q}")[64 * r:64 * r + 64, P * (k // 2):P * (k // 2) + P],
                                      p2T[:, S * b:S * b + S], U[:, b, :], start=True, stop=True)
                        last.then_inc(fulled(f"Ya_{q}"), 1)
                else:
                    for k in range(4, 11):
                        unit(e, k)
                for k in range(11, 16):
                    unit(e, k)
                if g is not None:
                    pe.wait_ge(xn_ready, 2 * g + 2)
                    four(g, "xnT2_0", xn, 0)
                    four(g, "xnT2_1", xn, 1)
                unit(e, 16)
                if g is not None:
                    for c in range(2):
                        wait_free(pe, g, f"QT_{c}")
                        pe.wait_ge(xnT_ready, 4 * g + 3 + c)
                        mm(ps(f"QT_{c}")[:], xwT[:, 0, :], xnT[:, 512 * c:512 * c + 512], start=True,
                           stop=True).then_inc(fulled(f"QT_{c}"), 1)
                unit(e, 17)
                if e is not None:
                    down_to(e, 17)
                if g is not None:
                    pe.wait_ge(Kx_ready, 2 * g + 2)
                    pe.wait_ge(V_ready, 4 * g + 4)
                    pe.wait_ge(Qx_ready, 2 * g + 2)
                    scores(g, 0)
                    scores(g, 1)
                    for t in range(T):
                        turn(g, t)
                        if t + 2 < T:
                            scores(g, t + 2)
                        values(g, t)
                        if t:
                            project(g, t - 1)

            def wait_free_unless(g, name, waited):
                before = att[place[name][4] - 4]
                if not before.startswith(waited + "_"):
                    wait_free(pe, g, name)

            run(pe, both)

        @block.scalar
        def _(act):
            cp = nc.scalar.copy
            for n, (kind, s) in enumerate(SETUP):
                act.wait_ge(setup_ps, n + 1)
                src = two[n % 3][:].rearrange("p (k d) -> p k d", d=P)
                if kind == "T":
                    cp(wT[:, 8 * s:8 * s + 8, :], src).then_inc(setup_cp, 1)
                elif kind == "W":
                    dst = (A1, A2, Wvo)[s // 2]
                    cp(dst[:, 8 * (s % 2):8 * (s % 2) + 8, :].rearrange("p (k r) d -> p r k d", r=2),
                       src.rearrange("p (r k) d -> p r k d", r=2)).then_inc(setup_cp, 1)
                else:
                    cp(xwT[:], src[:, 0:4, :])
                    cp(gwT[:], two[n % 3][:, 512:512 + E]).then_inc(setup_cp, 1)
            act.wait_ge(consts, 4)
            act.wait_ge(plane_ready, 1)
            act.wait_ge(loaded_m, 16 * 14)

            def moved(g, name, dst, ready, src=None):
                wait_full(act, g, name)
                cp(dst, ps(name)[:] if src is None else src).then_inc(ready, 1)

            def silu(e, k):
                if e is None:
                    return
                wait_full(act, e, f"H1_{k}")
                nc.scalar.activation(sil[:, k % 2, :], ps(f"H1_{k}")[:], ACT.Silu,
                                     bias=b1[:, pair[k]:pair[k] + 1]).then_inc(sil_ready, 1)

            def probs_moved(g, q):
                wait_full(act, g, f"p1T_{q}")
                src = ps(f"p1T_{q}")[:].rearrange("p (t h) -> p t h", h=HI)
                cp(p1T[0:64, :, 0, :], src[0:64])
                cp(p1T[64:128, :, 1, :], src[64:128]).then_inc(p1T_ready, 1)
                moved(g, f"p2T_{q}", p2T[:, 512 * q:512 * q + 512], p2T_ready)

            def PX_moved(g, q):
                for n in (2 * q, 2 * q + 1):
                    moved(g, f"PX_{n}", PX[:, 4 * n:4 * n + 4, :], PX_ready,
                          ps(f"PX_{n}")[:].rearrange("p (b h) -> p b h", h=HI))

            def V_moved(g, n):
                wait_full(act, g, f"V_{n}")
                src = ps(f"V_{n}")[:].rearrange("p (t a j r c) -> p t a j r c", t=2, a=2, r=2, c=XC)
                for r in range(2):
                    rr = slice(64 * r, 64 * r + 64)
                    for t in range(2):
                        last = cp(Vb[rr, 2 * n + t, :, :, XC * r:XC * r + XC],
                                  src[rr, t, :, :, r, :].rearrange("p a j c -> p j a c"))
                last.then_inc(V_ready, 1)

            def Q_moved(g, n):
                wait_full(act, g, f"QT_{n}")
                for q in range(4):
                    rr = slice(32 * q, 32 * q + 32)
                    last = cp(Qx[rr, q, 512 * n:512 * n + 512], ps(f"QT_{n}")[rr, :])
                last.then_inc(Qx_ready, 1)

            def both(e, g):
                if g is not None:
                    for n in range(2):
                        moved(g, f"ctxT_{n}", ctxT[:, 512 * n:512 * n + 512], ctxT_ready)
                    for n in range(2):
                        wait_full(act, g, f"KT_{n}")
                        for j in range(4):
                            last = nc.scalar.activation(Kx[:, j, 512 * n:512 * n + 512], ps(f"KT_{n}")[:], ACT.Copy,
                                                        scale=plane[:, j:j + 1])
                        last.then_inc(Kx_ready, 1)
                    V_moved(g, 0)
                    V_moved(g, 1)
                if e is not None:
                    for n in range(2):
                        moved(e, f"xnT3_{n}", xnT3[:, 512 * n:512 * n + 512], xnT3_ready)
                if g is not None:
                    V_moved(g, 2)
                    V_moved(g, 3)
                if e is not None:
                    act.wait_ge(dg_ready, e + 1)
                    nc.scalar.activation(gex[:], ga[:], ACT.Exp).then_inc(gex_ready, 1)
                if g is not None:
                    for n in range(2):
                        moved(g, f"xnT1_{n}", xnT[:, 512 * n:512 * n + 512], xnT_ready)
                silu(e, 0)
                if g is not None:
                    for n in range(8):
                        h0 = POOL * 4 * (n % 4)
                        moved(g, f"M_{n}", M[:, n // 4, :, h0:h0 + 4 * POOL].rearrange("p b (h i) -> p h b i", i=POOL),
                              M_ready, ps(f"M_{n}")[:].rearrange("p (h b i) -> p h b i", b=GB, i=POOL))
                if e is not None:
                    for n in range(2):
                        moved(e, f"combT_{n}", combT[:, 512 * n:512 * n + 512], combT_ready)
                    moved(e, "combS", combsT[:], combT_ready, ps("combS")[:].bitcast(bf16))
                for k in range(1, 5):
                    silu(e, k)
                if g is not None:
                    for q in range(Q):
                        act.wait_ge(d1_ready, 4 * g + 2 * q + 2)
                        nc.scalar.activation(e1[:, q], e1[:, q], ACT.Exp, scale=AGENT_SCALE).then_inc(e1_ready, 1)
                        act.wait_ge(d2_ready, 2 * g + q + 1)
                        nc.scalar.activation(e2[:, q], e2[:, q], ACT.Exp, scale=AGENT_SCALE).then_inc(e2_ready, 1)
                silu(e, 5)
                if g is not None:
                    probs_moved(g, 0)
                silu(e, 6)
                if g is not None:
                    PX_moved(g, 0)
                    probs_moved(g, 1)
                silu(e, 7)
                if g is not None:
                    PX_moved(g, 1)
                silu(e, 8)
                if g is not None:
                    for n in range(4):
                        h0 = POOL * 4 * n
                        moved(g, f"UT_{n}", UT[:, :, h0:h0 + 4 * POOL].rearrange("p b (h i) -> p h b i", i=POOL),
                              UT_ready, ps(f"UT_{n}")[:].rearrange("p (h b i) -> p h b i", b=GB, i=POOL))
                for k in range(9, 16):
                    silu(e, k)
                if g is not None:
                    for n in range(2):
                        moved(g, f"xnT2_{n}", xnT[:, 512 * n:512 * n + 512], xnT_ready)
                silu(e, 16)
                if g is not None:
                    Q_moved(g, 0)
                silu(e, 17)
                if g is not None:
                    Q_moved(g, 1)
                    for t in range(T + 1):
                        if t < T:
                            for k in (2 * t, 2 * t + 1):
                                act.wait_ge(dx_ready, 2 * T * g + k + 1)
                                nc.scalar.activation(pr[:, k % 4], pr[:, k % 4], ACT.Exp,
                                                     scale=X_SCALE).then_inc(pr_ready, 1)
                        if t:
                            for k in (2 * t - 2, 2 * t - 1):
                                if k >= 4 and k % 2 == 0:
                                    wait_full(act, g, f"OL_{k // 2 - 2}")
                                moved(g, f"PT_{k}", pT[:, k % 4], pT_ready,
                                      ps(f"PT_{k}")[:].rearrange("p (j q) -> p j q", q=P))

            run(act, both)

        @block.vector
        def _(dve):
            V = nc.vector
            dve.wait_ge(consts, 3)
            V.tensor_reduce(plane[:], planes[:], AX, ALU.add).then_inc(plane_ready, 1)
            dve.wait_ge(loaded_m, 16 * 14)
            links = {"a": 0, "e": 0}

            def link(ins, g, kind="a"):
                links[kind] += 1
                signal, per = (vec_a, LINKS_A) if kind == "a" else (vec_e, LINKS_E)
                ins.then_inc(signal, 1)
                dve.wait_ge(signal, per * g + links[kind])

            def norm(g, kind, src, dst, var, rstd_r, count, ready, between=lambda: None):
                for t in range(T):
                    last = V.bn_stats(stats[:, t, :], src[:, t, :])
                link(last, g, kind)
                even, odd = stats[:, :, 0:3], stats[:, :, 3:6]
                V.tensor_tensor(mean2[:], even[:, :, 1], odd[:, :, 1], ALU.add)
                V.tensor_tensor(diff[:], even[:, :, 1], odd[:, :, 1], ALU.subtract)
                link(V.tensor_tensor(sqd[:], even[:, :, 2], odd[:, :, 2], ALU.add), g, kind)
                V.tensor_scalar(mean[:], mean2[:], 0.5, None, ALU.mult)
                V.tensor_tensor(diff2[:], diff[:], diff[:], ALU.mult)
                link(V.tensor_scalar(sqd2[:], sqd[:], 1.0 / D, EPS, ALU.mult, ALU.add), g, kind)
                V.scalar_tensor_tensor(ve[:], diff2[:], 0.25, sqd2[:], ALU.mult, ALU.add).then_inc(var, 1)
                between()
                dve.wait_ge(rstd_r, count)
                for t in range(T):
                    last = V.tensor_scalar(dst[:, t, :], src[:, t, :], mean[:, t:t + 1], rstd[:, t:t + 1],
                                           ALU.subtract, ALU.mult)
                last.then_inc(ready, 1)

            def gate_shift(e):
                wait_full(dve, e, "gate")
                lg = ps("gate")[:, 0:T * E].rearrange("p (t e) -> p t e", e=E)
                link(V.tensor_reduce(g1[:], lg, AX, ALU.max), e, "e")
                V.tensor_tensor(ga[:], lg, g1[:].unsqueeze(2).to_broadcast([P, T, E]),
                                ALU.subtract).then_inc(dg_ready, 1)

            def gate(e):
                def link_e(ins):
                    link(ins, e, "e")

                te = [P, T, E]
                dve.wait_ge(gex_ready, e + 1)
                link_e(V.tensor_reduce(g3[:], gex[:], AX, ALU.add))
                link_e(V.reciprocal(g2[:], g3[:]))
                link_e(V.tensor_tensor(orig[:], gex[:], g2[:].unsqueeze(2).to_broadcast(te), ALU.mult))
                link_e(V.tensor_tensor(sc[:], orig[:], gb[:].unsqueeze(1).to_broadcast(te), ALU.add))
                sg = sc[:].rearrange("p t (g e) -> p (t g) e", e=EG)
                V.tensor_tensor(ps6[:, :, 0:2], sg[:, :, 0:2], sg[:, :, 2:4], ALU.add)
                V.tensor_tensor(ps6[:, :, 2:4], sg[:, :, 0:3:2], sg[:, :, 1:4:2], ALU.add)
                V.tensor_tensor(ps6[:, :, 4:5], sg[:, :, 0:1], sg[:, :, 3:4], ALU.add)
                link_e(V.tensor_tensor(ps6[:, :, 5:6], sg[:, :, 1:2], sg[:, :, 2:3], ALU.add))
                link_e(V.tensor_reduce(gs[:], ps6[:], AX, ALU.max))
                gsv = gs[:].rearrange("p (t g) -> p t g", g=EG)
                gg = [P, T, EG, EG]
                other, own = gsv.unsqueeze(2).to_broadcast(gg), gsv.unsqueeze(3).to_broadcast(gg)
                V.tensor_tensor(gta[:], other, own, ALU.is_gt)
                link_e(V.tensor_tensor(gtb[:], other, own, ALU.is_equal))
                link_e(V.tensor_tensor(gtb[:], gtb[:], lower[:].unsqueeze(1).to_broadcast(gg), ALU.mult))
                link_e(V.tensor_tensor(gta[:], gta[:], gtb[:], ALU.add))
                link_e(V.tensor_reduce(rank[:], gta[:].rearrange("p t a b -> p (t a) b"), AX, ALU.add))
                link_e(V.tensor_scalar(keep[:], rank[:], 2.0, None, ALU.is_lt))
                link_e(V.tensor_scalar(kb[:], keep[:], FAR, -FAR, ALU.mult, ALU.add))
                tg = tv[:].rearrange("p t (g e) -> p (t g) e", e=EG)
                ge = [P, T * EG, EG]
                link_e(V.tensor_tensor(tg, sg, keep[:].unsqueeze(2).to_broadcast(ge), ALU.mult))
                link_e(V.tensor_tensor(tg, tg, kb[:].unsqueeze(2).to_broadcast(ge), ALU.add))
                for k in range(2):
                    link_e(V.tensor_reduce(g1[:], tv[:], AX, ALU.max))
                    link_e(V.tensor_tensor(oh[:, k], tv[:], g1[:].unsqueeze(2).to_broadcast(te), ALU.is_equal))
                    link_e(V.tensor_tensor(oh[:, k], oh[:, k], down[:].unsqueeze(1).to_broadcast(te), ALU.mult))
                    link_e(V.tensor_reduce(g2[:], oh[:, k], AX, ALU.max))
                    link_e(V.tensor_tensor(oh[:, k], oh[:, k], g2[:].unsqueeze(2).to_broadcast(te), ALU.is_equal))
                    if k == 0:
                        link_e(V.scalar_tensor_tensor(tv[:], oh[:, 0], -FARTHER, tv[:], ALU.mult, ALU.add))
                link_e(V.tensor_tensor(tv[:], oh[:, 0], oh[:, 1], ALU.add))
                cw = comb[:, :, 0:E]
                link_e(V.tensor_tensor(cw, tv[:], orig[:], ALU.mult))
                link_e(V.tensor_copy(combs[:, :, 0:E], cw))
                link_e(V.tensor_tensor(tv[:], cw, combs[:, :, 0:E], ALU.subtract))
                link_e(V.tensor_copy(combs[:, :, E:2 * E], tv[:]))
                link_e(V.tensor_tensor(tv[:], tv[:], combs[:, :, E:2 * E], ALU.subtract))
                V.tensor_copy(combs[:, :, 2 * E:3 * E], tv[:]).then_inc(comb_ready, 1)

            def hidden(e, k):
                if e is None:
                    return
                wait_full(dve, e, f"H3_{k}")
                dve.wait_ge(sil_ready, UNITS * e + k + 1)
                p = pair[k]
                if k not in PAIRED:
                    V.scalar_tensor_tensor(hT[:, k % 2, :], ps(f"H3_{k}")[:], b3[:, p:p + 1],
                                           sil[:, k % 2, :], ALU.add, ALU.mult).then_inc(hT_ready, 1)
                    return
                V.scalar_tensor_tensor(hid[:, k % 2, :], ps(f"H3_{k}")[:], b3[:, p:p + 1],
                                       sil[:, k % 2, :], ALU.add, ALU.mult).then_inc(hid_ready, 1)
                dve.wait_ge(hid_ready, len(PAIRED) * e + PAIRED.index(k) + 1)
                wait_full(dve, e, f"C_{k}")
                V.tensor_tensor(hT[:, k % 2, :], hid[:, k % 2, :], ps(f"C_{k}")[:], ALU.mult).then_inc(hT_ready, 1)

            def result(e, c):
                if e is None:
                    return
                wait_full(dve, e, f"Y_{c}")
                V.tensor_tensor(xo[:, 4 * c:4 * c + 4, :], xe[:, 4 * c:4 * c + 4, :],
                                ps(f"Y_{c}")[:].rearrange("p (t d) -> p t d", d=D), ALU.add).then_inc(out_ready, 1)

            def soften(g, q):
                for n in (2 * q, 2 * q + 1):
                    wait_full(dve, g, f"s1_{n}")
                    s1 = ps(f"s1_{n}")[:].rearrange("p (b s) -> p b s", s=P)[:, :, 0:S]
                    link(V.tensor_reduce(m1[:, n], s1, AX, ALU.max), g)
                    V.tensor_tensor(e1[:, q, 4 * (n % 2):4 * (n % 2) + 4], s1,
                                    m1[:, n].unsqueeze(2).to_broadcast([P, 4, S]), ALU.subtract).then_inc(d1_ready, 1)
                wait_full(dve, g, f"s2_{q}")
                s2 = ps(f"s2_{q}")[:].rearrange("p (k i) -> p k i", i=POOL)
                link(V.tensor_reduce(m2[:], s2, AX, ALU.max), g)
                V.tensor_tensor(e2[:, q].rearrange("p t (h i) -> p (t h) i", i=POOL), s2,
                                m2[:].unsqueeze(2).to_broadcast([P, QT * H, POOL]), ALU.subtract).then_inc(d2_ready, 1)

            def normalise_2(g, q):
                dve.wait_ge(e2_ready, 2 * g + q + 1)
                e2v = e2[:, q].rearrange("p t (h i) -> p (t h) i", i=POOL)
                link(V.tensor_reduce(l2[:], e2v, AX, ALU.add), g)
                link(V.reciprocal(r2[:], l2[:]), g)
                V.tensor_tensor(e2v, e2v, r2[:].unsqueeze(2).to_broadcast([P, QT * H, POOL]),
                                ALU.mult).then_inc(p2_ready, 1)

            def sums_1(g, q):
                dve.wait_ge(e1_ready, 2 * g + q + 1)
                link(V.tensor_reduce(l1[:], e1[:, q], AX, ALU.add), g)
                link(V.reciprocal(r1[:, 8 * q:8 * q + 8], l1[:]), g)

            def softmax_in(g, t):
                for k in (2 * t, 2 * t + 1):
                    wait_full(dve, g, f"S_{k}")
                    sv = ps(f"S_{k}")[:].rearrange("p (h s) -> p h s", s=S)
                    link(V.tensor_reduce(mx[:, k % 2], sv, AX, ALU.max), g)
                    if k >= 4 and k % 2 == 0:
                        wait_full(dve, g, f"PT_{k - 3}")
                    V.tensor_tensor(pr[:, k % 4], sv, mx[:, k % 2].unsqueeze(2).to_broadcast([P, HALF, S]),
                                    ALU.subtract).then_inc(dx_ready, 1)

            def normalise(g, t):
                name = f"OL_{t}"
                wait_full(dve, g, name)
                link(V.reciprocal(rl[:], ps(name)[:, 256:512]), g, "a" if t < T - 1 else "e")
                V.tensor_tensor(On[:, t % 2].rearrange("p s q -> p (s q)"), ps(name)[:, 0:256], rl[:],
                                ALU.mult).then_inc(On_ready, 1)

            def add_x(g, t):
                wait_full(dve, g, f"Yx_{t}")
                V.tensor_tensor(xe[:, t, :], xr[:, t, :], ps(f"Yx_{t}")[:, 0:P], ALU.add).then_inc(xattn_added, 1)

            def both(e, g):
                links["a"] = links["e"] = 0
                if e is not None:
                    normalise(e, T - 1)
                    add_x(e, T - 2)
                    add_x(e, T - 1)
                    dve.wait_ge(xattn_added, T * e + T)
                    norm(e, "e", xe, xn3, var3_ready, rstd3_ready, e + 1, xn3_ready)
                if g is not None:
                    dve.wait_ge(x_loaded, 16 * g + 16)
                    norm(g, "a", xin, xn, var_ready, rstd_ready, 2 * g + 1, xn_ready)
                if e is not None:
                    gate_shift(e)
                if g is not None:
                    dve.wait_ge(xnT_ready, 4 * g + 2)
                    V.tensor_reduce(pooled[:], xnT[:, 0:TOK].rearrange("p (k s) -> p k s", s=S // POOL), AX,
                                    ALU.add).then_inc(pooled_ready, 1)
                if e is not None:
                    gate(e)
                if g is not None:
                    soften(g, 0)
                for k in range(0, 4):
                    hidden(e, k)
                if g is not None:
                    soften(g, 1)
                    hidden(e, 4)
                    normalise_2(g, 0)
                    hidden(e, 5)
                    normalise_2(g, 1)
                    hidden(e, 6)
                    for q in range(Q):
                        sums_1(g, q)
                    for k in (7, 8, 9):
                        hidden(e, k)
                    result(e, 0)
                    for n in range(4):
                        wait_full(dve, g, f"U_{n}")
                        V.tensor_tensor(U[:, 4 * n:4 * n + 4, :], ps(f"U_{n}")[:].rearrange("p (b d) -> p b d", d=D),
                                        r1[:, 4 * n:4 * n + 4].unsqueeze(2).to_broadcast([P, 4, D]),
                                        ALU.mult).then_inc(U_ready, 1)
                    hidden(e, 10)
                    dve.wait_ge(xr_ready, g + 1)
                    for q in range(Q):
                        wait_full(dve, g, f"Ya_{q}")
                        V.tensor_tensor(xr[:, 4 * q:4 * q + 4, :], xr[:, 4 * q:4 * q + 4, :],
                                        ps(f"Ya_{q}")[:].rearrange("p (t d) -> p t d", d=D),
                                        ALU.add).then_inc(attn_added, 1)
                    dve.wait_ge(attn_added, 2 * g + 2)
                    norm(g, "a", xr, xn, var_ready, rstd_ready, 2 * g + 2, xn_ready, lambda: hidden(e, 11))
                else:
                    for k in range(4, 10):
                        hidden(e, k)
                    result(e, 0)
                    for k in range(10, 12):
                        hidden(e, k)
                for k in range(12, 18):
                    hidden(e, k)
                result(e, 1)
                if g is not None:
                    for t in range(T + 1):
                        if t < T:
                            softmax_in(g, t)
                        if t >= 2:
                            normalise(g, t - 2)
                        if t >= 3:
                            add_x(g, t - 3)
                    assert links["a"] == LINKS_A, links
                if e is not None:
                    dve.wait_ge(stored, 16 * CHUNKS * (e + 1))
                    assert links["e"] == LINKS_E, links

            run(dve, both)


_INS = ['x', 'ctx_1024', 'L0_attn_Wqkv', 'L0_attn_Wo', 'L0_attn_bo', 'L0_xattn_Wq', 'L0_xattn_Wk', 'L0_xattn_Wv',
        'L0_xattn_Wo', 'L0_ffn_gate_w', 'L0_ffn_gate_b', 'L0_ffn_We1', 'L0_ffn_be1', 'L0_ffn_We2', 'L0_ffn_be2',
        'L0_ffn_We3', 'L0_ffn_be3', 'L0_ffn_ws1', 'L0_ffn_bs1', 'L0_ffn_ws2', 'L0_ffn_bs2', 'L0_ffn_ws3', 'L0_ffn_bs3']


def kernel(**inputs):
    import concourse.bacc as bacc
    from concourse.bass_utils import run_bass_kernel_spmd

    nc = bacc.Bacc("TRN2", target_bir_lowering=False, num_devices=1)
    arrays, args = {}, []
    for name in _INS:
        a = np.ascontiguousarray(inputs[name])
        arrays[f"in_{name}"] = a
        args.append(nc.dram_tensor(f"in_{name}", a.shape, mybir.dt.from_np(a.dtype), kind="ExternalInput").ap())
    out = nc.dram_tensor("out_x", arrays["in_x"].shape, mybir.dt.float32, kind="ExternalOutput").ap()
    decoder_block(nc, *args, out)
    r = run_bass_kernel_spmd(nc, [arrays], core_ids=[0])
    return r.results[0]["out_x"]
```

```python
import numpy as np
import concourse.bass as bass
from concourse import mybir
from contextlib import ExitStack


def decoder_block(nc, x, ctx_in, Wqkv, Wo_a, bo, Wq, Wk, Wv, Wo_x, gate_w, gate_b,
                  We1, be1, We2, be2, We3, be3, ws1, bs1, ws2, bs2, ws3, bs3, out):
    fp32, bf16, fp32r = mybir.dt.float32, mybir.dt.bfloat16, mybir.dt.float32r
    ALU, ACT, AX = mybir.AluOpType, mybir.ActivationFunctionType, mybir.AxisListType.X

    B, S, D = x.shape
    P = 128
    GB = 16
    GROUPS = B // GB
    TOK = GB * S
    T = TOK // P
    QT = 4
    Q = T // QT
    H, POOL, DH = 16, 8, 64
    HI = H * POOL
    XH, XC = 16, 8
    HALF = XH // 2
    E, EG, EI = 16, 4, 64
    EP = E // 2
    CH = 512
    CHUNKS = TOK // CH
    EPS = 1e-5
    AGENT_SCALE = DH ** -0.5 / (S // POOL)
    X_SCALE = XC ** -0.5
    MASKED = -1e9
    FAR, FARTHER = 1e30, 1e32

    x_v = x.rearrange("(g b) s d -> g (b s) d", b=GB).rearrange("g (t p) d -> g p t d", p=P)
    c_v = ctx_in.rearrange("(g b) s d -> g (b s) d", b=GB).rearrange("g (t p) d -> g p t d", p=P)
    o_v = out.rearrange("(g b) s d -> g (b s) d", b=GB).rearrange("g (t p) d -> g p t d", p=P)

    att = ["ctxT_0", "ctxT_1", "V_0", "V_1", "xnT1_0", "xnT1_1", "V_2", "V_3", "KT_0"]
    att += [f"M_{n}" for n in range(8)]
    att += ["s1_0", "s1_1", "s2_0", "KT_1", "s1_2", "s1_3", "s2_1"]
    att += ["p1T_0", "p2T_0", "PX_0", "PX_1", "p1T_1", "p2T_1", "PX_2", "PX_3"]
    att += [f"UT_{n}" for n in range(4)] + [f"U_{n}" for n in range(4)] + ["Ya_0", "Ya_1"]
    att += ["xnT2_0", "xnT2_1", "QT_0", "QT_1"] + [f"S_{n}" for n in range(2 * T)]
    UNITS = CHUNKS * (EP + 1)
    PAIRED = [k for k in range(UNITS) if k % (EP + 1)]
    pair = [k % (EP + 1) - 1 if k % (EP + 1) else EP for k in range(UNITS)]
    RINGS = {"att": (att, 4),
             "h1": (["xnT3_0"] + [f"H1_{k}" for k in range(UNITS)], 1),
             "h3": (["xnT3_1"] + [f"H3_{k}" for k in range(UNITS)], 1),
             "c": (["gate", "combS"] + [f"C_{k}" for k in PAIRED if k < EP + 1] + ["combT_0", "combT_1"]
                   + [f"C_{k}" for k in PAIRED if k > EP], 1),
             "y": (["Y_0", "Y_1"], 1),
             "pt": ([f"PT_{n}" for n in range(2 * T)], 2),
             "ol": ([f"OL_{t}" for t in range(T)], 1),
             "yx": ([f"Yx_{t}" for t in range(T)], 1)}
    place = {}
    for ring, (names, n) in RINGS.items():
        for at, name in enumerate(names):
            k = at % n
            place[name] = (ring, k, at // n, len(range(k, len(names), n)), at)

    with ExitStack() as ctx:
        def sb(name, shape, dt=fp32):
            return ctx.enter_context(nc.sbuf_tensor(name, shape, dt))

        def sem(name):
            return ctx.enter_context(nc.semaphore(name))

        KQ = sb("KQ", [P, 8, TOK])
        Kx, Qx = KQ[:, 0:4, :], KQ[:, 4:8, :]
        wqkv = KQ[:, 0:3, :].rearrange("p a n -> p (a n)")
        wT = KQ[:, 3:6, :].rearrange("p a (b n) -> p (a b) n", n=P)
        woa = KQ[:, 6:7, :].rearrange("p a (b n) -> p (a b) n", n=D)
        w1, w3 = [wqkv[:, n * EI * (E + 2):(n + 1) * EI * (E + 2)].rearrange("p (e i) -> p e i", i=EI)
                  for n in range(2)]
        xw = KQ[:, 7, 0:512].rearrange("p (a n) -> p a n", n=D)
        gw = KQ[0:E, 7, 512:512 + D]
        A1 = sb("A1", [P, H, D])
        A2 = sb("A2", [P, H, D])
        Wvo = sb("Wvo", [P, H, D])
        xwT = sb("xwT", [P, 4, D])
        woM = sb("woM", [P, 2, 2, D])
        w1h = sb("w1h", [P, E + 2, EI], fp32r)
        w3h = sb("w3h", [P, E + 2, EI], fp32r)
        w1l = sb("w1l", [P, E + 2, EI], fp32r)
        w3l = sb("w3l", [P, E + 2, EI], fp32r)
        w2 = sb("w2", [P, EP + 1, D])
        b1 = sb("b1", [P, EP + 1])
        b3 = sb("b3", [P, EP + 1])
        b2x = sb("b2x", [P, D])
        gwT = sb("gwT", [P, E])
        gb = sb("gb", [P, E])
        bo_b = sb("bo_b", [P, D])
        ident = sb("ident", [P, P])
        identb = sb("identb", [P, P], bf16)
        maskb = sb("maskb", [P, HALF, S], bf16)
        planes = sb("planes", [P, 4, 4])
        plane = sb("plane", [P, 4])
        onehot3 = sb("onehot3", [P, E], bf16)
        spread = sb("spread", [P, EP, 2, EI], bf16)
        down = sb("down", [P, E])
        mhalf = sb("mhalf", [P, T])
        xin = sb("xin", [P, T, D])
        cin = sb("cin", [P, T, D])
        xr = sb("xr", [P, T, D])
        xe = sb("xe", [P, T, D])
        xn = sb("xn", [P, T, D])
        xn3 = sb("xn3", [P, T, D])
        xo = xn3
        xnT = sb("xnT", [P, TOK + S])
        xnT3 = sb("xnT3", [P, TOK])
        xnT3h = sb("xnT3h", [P, TOK], fp32r)
        xnT3l = sb("xnT3l", [P, TOK], fp32r)
        stats = {kind: sb(f"stats_{kind}", [P, T, 6]) for kind in "ae"}
        norms = {kind: [sb(f"norm_{kind}{k}", [P, T]) for k in range(8)] for kind in "ae"}
        (va, rstda), (vb, rstdb) = norms["a"][6:], norms["e"][6:]
        pooled = sb("pooled", [P, GB * POOL])
        M = sb("M", [P, 2, GB, HI])
        e1 = sb("e1", [P, Q, 8, S])
        m1 = sb("m1", [P, 4, 4])
        l1 = sb("l1", [P, 8])
        r1 = sb("r1", [P, GB])
        m2 = sb("m2", [P, QT * H])
        l2 = sb("l2", [P, QT * H])
        r2 = sb("r2", [P, QT * H])
        p1T = sb("p1T", [P, QT, 2, HI])
        PXUT = sb("PXUT", [P, 2, GB, HI])
        PX, UT = PXUT[:, 0], PXUT[:, 1]
        U = PX
        e2 = UT[:, QT * Q:GB].rearrange("p (q t) h -> p q t h", q=Q)
        p2T = M[:, 1, 0:TOK // HI, :].rearrange("p b h -> p (b h)")
        diag_q, diag_k = [X.rearrange("p b h -> p (b h)").rearrange("p (a c) -> p a c", c=2 * D) for X in (PX, UT)]
        diag_o = M[:, 0].rearrange("p b h -> p (b h)").rearrange("p (a c) -> p a c", c=2 * D)
        ctxT = sb("ctxT", [P, TOK])
        Vb = sb("Vb", [P, T, XH // 2, 2, 2 * XC])
        mx = sb("mx", [P, 4, HALF])
        lx = sb("lx", [P, 4, HALF])
        rx = sb("rx", [P, 4, HALF])
        PR = 2 * QT
        pr = PXUT[:].rearrange("p a b h -> p (a b h)").rearrange("p (k h s) -> p k h s", k=PR, s=S)
        pT = M[:, 0].rearrange("p b h -> p (b h)").rearrange("p (k j q) -> p k j q", k=4, q=P)
        On = sb("On", [P, 2, 2, P])
        g1 = sb("g1", [P, T])
        g2 = sb("g2", [P, T])
        g3 = sb("g3", [P, T])
        gs = sb("gs", [P, T * EG])
        rank = sb("rank", [P, T * EG])
        kb = sb("kb", [P, T * EG])
        ga, gex, orig, sc, tv = [sb(f"gate{k}", [P, T, E]) for k in range(5)]
        beats = sb("beats", [P, T, EG, EG])
        ps6 = sb("ps6", [P, T * EG, 6])
        oh = sb("oh", [P, 2, T, E])
        comb = sb("comb", [P, T, 2 * E])
        combs = sb("combs", [P, T, P], bf16)
        combT = sb("combT", [P, TOK])
        combsT = sb("combsT", [P, TOK], bf16)
        sil = sb("sil", [P, 2, CH])
        hT = sb("hT", [P, 2, CH])

        two = [ctx.enter_context(nc.psum_tensor(f"banks{k}", [P, 1024], fp32)) for k in range(4)]
        banks = [two[k // 2][:, 512 * (k % 2):512 * (k % 2) + 512] for k in range(8)]
        bank = {"att": banks[0:4], "h1": banks[4:5], "h3": banks[5:6], "c": banks[6:7], "y": banks[7:8],
                "pt": banks[4:6], "ol": banks[6:7], "yx": banks[7:8]}

        full = {(r, k): sem(f"{r}{k}_full") for r, (_, n) in RINGS.items() for k in range(n)}

        loaded_q = [sem(f"loaded_q{s}") for s in range(3)]
        loaded_x, loaded_w, loaded_e, loaded_m = sem("loaded_x"), sem("loaded_w"), sem("loaded_e"), sem("loaded_m")
        diag_cleared, diag_ready, spread_wo = sem("diag_cleared"), sem("diag_ready"), sem("spread_wo")
        const_step, consts, plane_ready = sem("const_step"), sem("consts"), sem("plane_ready")
        setup_ps, setup_cp = sem("setup_ps"), sem("setup_cp")
        x_loaded, c_loaded, xr_ready = sem("x_loaded"), sem("c_loaded"), sem("xr_ready")
        var_ready, rstd_ready, xn_ready, xnT_ready = (
            sem("var_ready"), sem("rstd_ready"), sem("xn_ready"), sem("xnT_ready"))
        var3_ready, rstd3_ready, xn3_ready, xnT3_ready = (
            sem("var3_ready"), sem("rstd3_ready"), sem("xn3_ready"), sem("xnT3_ready"))
        w_split, hi_ready, lo_ready = sem("w_split"), sem("hi_ready"), sem("lo_ready")
        ctxT_ready, Kx_ready, V_ready = sem("ctxT_ready"), sem("Kx_ready"), sem("V_ready")
        pooled_ready, M_ready = sem("pooled_ready"), sem("M_ready")
        d1_ready, d2_ready, e1_ready, e2_ready = sem("d1_ready"), sem("d2_ready"), sem("e1_ready"), sem("e2_ready")
        p2_ready, p1T_ready, p2T_ready = sem("p2_ready"), sem("p1T_ready"), sem("p2T_ready")
        PX_ready, UT_ready, U_ready, attn_added = sem("PX_ready"), sem("UT_ready"), sem("U_ready"), sem("attn_added")
        Qx_ready, mx_ready, dx_ready, pr_ready = sem("Qx_ready"), sem("mx_ready"), sem("dx_ready"), sem("pr_ready")
        rx_ready, pn_ready, pT_ready = sem("rx_ready"), sem("pn_ready"), sem("pT_ready")
        On_ready, xattn_added = sem("On_ready"), sem("xattn_added")
        dg_ready, gex_ready, comb_ready, combT_ready = (
            sem("dg_ready"), sem("gex_ready"), sem("comb_ready"), sem("combT_ready"))
        sil_ready, hid_ready, hT_ready = sem("sil_ready"), sem("hid_ready"), sem("hT_ready")
        out_ready, stored = sem("out_ready"), sem("stored")
        vec_a, vec_e = sem("vec_a"), sem("vec_e")
        LINKS_A, LINKS_E = 44, 28

        read = {"gate": (dg_ready, 1, 0), "combS": (combT_ready, 3, 0), "combT_0": (combT_ready, 3, 1),
                "combT_1": (combT_ready, 3, 2)}
        for n in range(2):
            read |= {f"xnT1_{n}": (xnT_ready, 4, n), f"xnT2_{n}": (xnT_ready, 4, 2 + n),
                     f"xnT3_{n}": (hi_ready, 2, n), f"ctxT_{n}": (ctxT_ready, 2, n), f"KT_{n}": (Kx_ready, 2, n),
                     f"QT_{n}": (Qx_ready, 2, n), f"Y_{n}": (out_ready, 2, n), f"s2_{n}": (d2_ready, 2, n),
                     f"p1T_{n}": (p1T_ready, 2, n), f"p2T_{n}": (p2T_ready, 2, n), f"Ya_{n}": (attn_added, 2, n)}
        for n in range(4):
            read |= {f"V_{n}": (V_ready, 4, n), f"s1_{n}": (d1_ready, 4, n), f"PX_{n}": (PX_ready, 4, n),
                     f"UT_{n}": (UT_ready, 4, n), f"U_{n}": (U_ready, 4, n)}
        for n in range(8):
            read |= {f"M_{n}": (M_ready, 8, n)}
        for n in range(2 * T):
            read |= {f"S_{n}": (dx_ready, T, n // 2) if n % 2 else (pr_ready, 2 * T, n),
                     f"PT_{n}": (pT_ready, 2 * T, n)}
        for t in range(T):
            read |= {f"OL_{t}": (On_ready, T, t), f"Yx_{t}": (xattn_added, T, t)}
        for k in range(UNITS):
            read[f"H1_{k}"] = (sil_ready, UNITS, k)
            if k in PAIRED:
                read |= {f"H3_{k}": (hid_ready, len(PAIRED), PAIRED.index(k)), f"C_{k}": (hT_ready, UNITS, k)}
            else:
                read[f"H3_{k}"] = (hT_ready, UNITS, k)

        block = ctx.enter_context(nc.Block())

        def ps(name):
            return bank[place[name][0]][place[name][1]]

        def wait_free(pe, g, name):
            ring, k, use, _, at = place[name]
            if use:
                signal, per, n = read[RINGS[ring][0][at - RINGS[ring][1]]]
                pe.wait_ge(signal, g * per + n + 1)
            elif ring == "yx":
                pe.wait_ge(out_ready, CHUNKS * g)
            elif ring == "att" and k % 2 == 0:
                pe.wait_ge(pr_ready, 2 * T * g)

        def wait_full(eng, g, name):
            ring, k, use, per, _ = place[name]
            eng.wait_ge(full[ring, k], g * per + use + 1)

        def fulled(name):
            return full[place[name][:2]]

        def run(eng, both):
            both(None, 0)
            with eng.Fori(0, GROUPS - 1) as e:
                both(e, e + 1)
            both(GROUPS - 1, None)

        SETUP = [("T", 0), ("X", 0), ("T", 1), ("T", 2)] + [("W", s) for s in range(6)]

        @block.sync
        def _(sp):
            for s in range(3):
                third = slice(H * DH * s, H * DH * s + H * DH)
                sp.dma_start(wqkv[:, third], Wqkv[:, third]).then_inc(loaded_q[s], 16)
            sp.dma_start(woa, Wo_a.rearrange("(b p) d -> p b d", p=P)).then_inc(loaded_w, 16)
            sp.dma_start(xin[:], x_v[0]).then_inc(x_loaded, 16)
            sp.dma_start(cin[:], c_v[0]).then_inc(c_loaded, 16)
            sp.dma_start(gb[:], gate_b.partition_broadcast(P)).then_inc(loaded_m, 16)
            sp.dma_start(bo_b[:], bo.partition_broadcast(P)).then_inc(loaded_m, 16)
            sp.dma_start(w2[:, 0:EP, :], We2.rearrange("(p a) i d -> (a i) p d", a=2)).then_inc(loaded_m, 16)
            sp.dma_start(w2[:, EP, :], ws2).then_inc(loaded_m, 16)
            with nc.allow_non_contiguous_dma("biases, a column each, once"):
                for b_sb, be, bs in ((b1, be1, bs1), (b3, be3, bs3)):
                    sp.dma_start(b_sb[:, 0:EP], be.rearrange("(p a) i -> (a i) p", a=2)).then_inc(loaded_m, 16)
                    sp.dma_start(b_sb[:, EP:EP + 1], bs.rearrange("(p a) -> p a", a=1)).then_inc(loaded_m, 16)
            sp.wait_ge(consts, 1)
            sp.dma_start(b2x[0:E, :], be2).then_inc(loaded_m, 16)
            sp.dma_start(b2x[E:E + 1, :], bs2.rearrange("(a d) -> a d", a=1)).then_inc(loaded_m, 16)
            sp.wait_ge(consts, 3)
            sp.wait_ge(setup_cp, 2)
            for s in range(2):
                for b in range(2):
                    for gq in range(4):
                        sp.dma_start(woM[32 * gq + 16 * b:32 * gq + 16 * b + 16, s, b, :],
                                     xwT[64 * s + 16 * gq:64 * s + 16 * gq + 16, 3, :]).then_inc(spread_wo, 16)
            sp.wait_ge(setup_cp, 4)
            for w_sb, we, ws in ((w1, We1, ws1), (w3, We3, ws3)):
                sp.dma_start(w_sb[:, 0:E, :], we.rearrange("e d i -> d e i")).then_inc(loaded_e, 16)
                sp.dma_start(w_sb[:, E:E + 2, :], ws.rearrange("d (e i) -> d e i", i=EI)).then_inc(loaded_e, 16)
            with sp.Fori(1, GROUPS) as g:
                sp.wait_ge(xr_ready, g)
                sp.dma_start(xin[:], x_v[bass.ds(g, 1)].rearrange("a p t d -> (a p) t d")).then_inc(x_loaded, 16)
                sp.wait_ge(ctxT_ready, 2 * g)
                sp.dma_start(cin[:], c_v[bass.ds(g, 1)].rearrange("a p t d -> (a p) t d")).then_inc(c_loaded, 16)

        @block.gpsimd
        def _(pool):
            steps = [0]

            def step(ins):
                steps[0] += 1
                ins.then_inc(const_step, 1)
                pool.wait_ge(const_step, steps[0])

            step(nc.gpsimd.memset(b2x[:], 0.0))
            nc.gpsimd.memset(mhalf[:], -0.5).then_inc(consts, 1)
            nc.gpsimd.memset(ident[:], 0.0)
            nc.gpsimd.memset(onehot3[:], 0.0)
            nc.gpsimd.memset(maskb[:], 0.0)
            nc.gpsimd.memset(beats[:], 0.0)
            step(nc.gpsimd.memset(planes[:], X_SCALE))
            step(nc.gpsimd.affine_select(out=ident[:], in_=ident[:], compare_op=ALU.not_equal, fill=1.0, base=0,
                                         pattern=[[-1, P]], channel_multiplier=1))
            nc.gpsimd.tensor_copy(identb[:], ident[:]).then_inc(consts, 1)
            nc.gpsimd.memset(woM[:], 0.0)
            nc.gpsimd.memset(p1T[:], 0.0)
            nc.gpsimd.memset(Vb[:], 0.0)
            nc.gpsimd.memset(xnT[:, TOK:TOK + S], 0.0)
            nc.gpsimd.memset(combs[:], 0.0)
            nc.gpsimd.memset(combT[:], 0.0)
            step(nc.gpsimd.memset(comb[:], 0.0))
            nc.gpsimd.memset(comb[:, :, E:E + 1], 1.0)
            nc.gpsimd.iota(down[:], pattern=[[-1, E]], base=E, channel_multiplier=0,
                           allow_small_or_imprecise_dtypes=True)
            for k in range(3):
                step(nc.gpsimd.affine_select(out=onehot3[:], in_=onehot3[:], compare_op=ALU.not_equal, fill=1.0,
                                             base=-E * k, pattern=[[-1, E]], channel_multiplier=1))
            step(nc.gpsimd.affine_select(out=planes[:], in_=planes[:], compare_op=ALU.is_ge, fill=0.0, base=0,
                                         pattern=[[-XC, 4], [-4 * XC, 4]], channel_multiplier=1))
            step(nc.gpsimd.affine_select(out=planes[:], in_=planes[:], compare_op=ALU.is_ge, fill=0.0, base=XC - 1,
                                         pattern=[[XC, 4], [4 * XC, 4]], channel_multiplier=-1))
            for r in range(2):
                rr = slice(64 * r, 64 * r + 64)
                step(nc.gpsimd.affine_select(out=maskb[rr], in_=maskb[rr], compare_op=ALU.is_ge, fill=MASKED, base=0,
                                             pattern=[[0, HALF], [-1, S]], channel_multiplier=1))
            nc.gpsimd.tensor_copy(spread[:].rearrange("r p a i -> r (p a) i"),
                                  onehot3[:].unsqueeze(2).to_broadcast([P, E, EI])).then_inc(consts, 1)

            def store(e, c):
                pool.wait_ge(out_ready, CHUNKS * e + c + 1)
                dst = o_v[e] if isinstance(e, int) else o_v[bass.ds(e, 1)].rearrange("a p t d -> (a p) t d")
                pool.dma_start(dst[:, QT * c:QT * c + QT, :], xo[:, QT * c:QT * c + QT, :]).then_inc(stored, 16)

            def both(e, g):
                if g is not None:
                    pool.wait_ge(var_ready, 2 * g + 1)
                    nc.gpsimd.tensor_tensor(rstda[:], va[:], mhalf[:], ALU.pow).then_inc(rstd_ready, 1)
                if e is not None:
                    pool.wait_ge(var3_ready, e + 1)
                    nc.gpsimd.tensor_tensor(rstdb[:], vb[:], mhalf[:], ALU.pow).then_inc(rstd3_ready, 1)
                    for n in range(2):
                        half = slice(512 * n, 512 * n + 512)
                        pool.wait_ge(hi_ready, 2 * e + n + 1)
                        nc.gpsimd.tensor_tensor(xnT3l[:, half], xnT3[:, half], xnT3h[:, half].bitcast(fp32),
                                                ALU.subtract).then_inc(lo_ready, 1)
                if g is not None:
                    pool.wait_ge(xn_ready, 2 * g + 1)
                    if e is not None:
                        pool.wait_ge(xattn_added, T * g)
                    else:
                        pool.wait_ge(loaded_m, 16 * 10)
                    nc.gpsimd.tensor_tensor(xr[:], xin[:], bo_b[:].unsqueeze(1).to_broadcast([P, T, D]),
                                            ALU.add).then_inc(xr_ready, 1)
                    if e is None:
                        pool.wait_ge(setup_cp, len(SETUP))
                        nc.gpsimd.memset(Qx, 0.0).then_inc(consts, 1)
                if e is not None:
                    store(e, 0)
                if g is not None:
                    pool.wait_ge(var_ready, 2 * g + 2)
                    nc.gpsimd.tensor_tensor(rstda[:], va[:], mhalf[:], ALU.pow).then_inc(rstd_ready, 1)
                if e is not None:
                    store(e, 1)
                if g is not None:
                    for k in range(2 * T):
                        pool.wait_ge(rx_ready, 2 * T * g + k + 1)
                        p = pr[:, k % PR]
                        nc.gpsimd.tensor_tensor(p, p, rx[:, k % 4].unsqueeze(2).to_broadcast([P, HALF, S]),
                                                ALU.mult).then_inc(pn_ready, 1)

            run(pool, both)
            pool.wait_ge(stored, 16 * CHUNKS * GROUPS)

        @block.tensor
        def _(pe):
            mm, turn_over = nc.tensor.matmul, nc.tensor.transpose
            pe.wait_ge(consts, 2)
            for n, (kind, s) in enumerate(SETUP):
                dst = two[n % 3]
                if n >= 3:
                    pe.wait_ge(setup_cp, n - 2)
                if kind == "T":
                    pe.wait_ge(loaded_q[s], 16)
                    for k in range(8):
                        c0 = (8 * s + k) * P
                        last = turn_over(dst[:, P * k:P * k + P], wqkv[:, c0:c0 + P], ident[:])
                elif kind == "W":
                    if s == 0:
                        pe.wait_ge(setup_cp, 4)
                    if s == 4:
                        pe.wait_ge(diag_ready, 2)
                    for k in range(4):
                        h2 = 4 * (s % 2) + k
                        a = wT[:, (0, 0, 16)[s // 2] + h2, :]
                        b = (diag_k, diag_q, diag_o)[s // 2][:, h2, :]
                        last = mm(dst[:, 256 * k:256 * k + 256], a, b, start=True, stop=True)
                else:
                    pe.wait_ge(loaded_x, 16 * 5)
                    for k in range(4):
                        turn_over(dst[:, P * k:P * k + P], xw[:, k, :], ident[:])
                    last = turn_over(dst[:, 512:512 + E], gw, ident[0:E, 0:E])
                last.then_inc(setup_ps, 1)
            pe.wait_ge(setup_cp, len(SETUP))
            pe.wait_ge(consts, 3)

            def four(g, name, src, n):
                wait_free(pe, g, name)
                for t in range(4):
                    last = turn_over(ps(name)[:, P * t:P * t + P], src[:, 4 * n + t, :], ident[:])
                last.then_inc(fulled(name), 1)

            def turn_comb(e, c):
                name = f"combT_{c}"
                wait_free(pe, e, name)
                for t in range(4):
                    last = turn_over(ps(name)[0:2 * E, P * t:P * t + P], comb[:, 4 * c + t, :], ident[:])
                last.then_inc(fulled(name), 1)

            def up(e, k):
                c = k // (EP + 1)
                t0, p = CH * c, pair[k]
                if k % (EP + 1) == 0:
                    pe.wait_ge(lo_ready, 2 * e + c + 1)
                xh, xl = xnT3h[:, t0:t0 + CH], xnT3l[:, t0:t0 + CH]
                for ring, wh, wl in (("H1", w1h, w1l), ("H3", w3h, w3l)):
                    name = f"{ring}_{k}"
                    wait_free(pe, e, name)
                    mm(ps(name)[:], wh[:, 2 * p:2 * p + 2, :], xl, start=True, stop=False)
                    mm(ps(name)[:], wl[:, 2 * p:2 * p + 2, :], xh, start=False, stop=False)
                    mm(ps(name)[:], wh[:, 2 * p:2 * p + 2, :], xh, start=False, stop=True).then_inc(fulled(name), 1)

            def weight(e, k):
                name = f"C_{k}"
                c = k // (EP + 1)
                wait_free(pe, e, name)
                mm(ps(name)[:], spread[:, pair[k], :, :], combsT[:, CH * c:CH * c + CH], start=True,
                   stop=True).then_inc(fulled(name), 1)

            def down_to(e, k):
                c, n = k // (EP + 1), k % (EP + 1)
                name = f"Y_{c}"
                if n == 0:
                    wait_free(pe, e, name)
                pe.wait_ge(hT_ready, UNITS * e + k + 1)
                for t in range(4):
                    mm(ps(name)[:, P * t:P * t + P], hT[:, k % 2, P * t:P * t + P], w2[:, pair[k], :],
                       start=(n == 0 and t == 0), stop=False, skip_group_check=True)
                if n == EP:
                    pe.wait_ge(combT_ready, 3 * e + 2 + c)
                    for t in range(4):
                        t0 = CH * c + P * t
                        last = mm(ps(name)[:, P * t:P * t + P], combT[:, t0:t0 + P], b2x[:],
                                  start=False, stop=True, skip_group_check=True)
                    last.then_inc(fulled(name), 1)

            def unit(e, k):
                if e is None:
                    return
                up(e, k)
                if k in PAIRED:
                    weight(e, k)
                if k == EP + 1:
                    turn_comb(e, 0)
                if k:
                    down_to(e, k - 1)
                if k == EP + 1:
                    turn_comb(e, 1)

            def scores_1(g, n):
                name = f"s1_{n}"
                wait_free(pe, g, name)
                if n == 0:
                    pe.wait_ge(M_ready, 8 * g + 4)
                for k in range(4):
                    b = 4 * n + k
                    last = mm(ps(name)[:, P * k:P * k + P], M[:, 0, b, :], xnT[:, S * b:S * b + P],
                              start=True, stop=True)
                last.then_inc(fulled(name), 1)

            def scores_2(g, q):
                name = f"s2_{q}"
                wait_free(pe, g, name)
                if q == 0:
                    pe.wait_ge(M_ready, 8 * g + 8)
                for k in range(8):
                    b, r = 8 * q + k, k % 2
                    last = mm(ps(name)[64 * r:64 * r + 64, P * (k // 2):P * (k // 2) + P],
                              xnT[:, S * b:S * b + S], M[:, 1, b, :], start=True, stop=True)
                last.then_inc(fulled(name), 1)

            def turn_probs(g, q):
                name = f"p1T_{q}"
                wait_free(pe, g, name)
                pe.wait_ge(e1_ready, 2 * g + q + 1)
                for t in range(4):
                    last = turn_over(ps(name)[:, P * t:P * t + P],
                                     e1[:, q, 2 * t:2 * t + 2, :].rearrange("p b s -> p (b s)"), ident[:])
                last.then_inc(fulled(name), 1)
                name = f"p2T_{q}"
                wait_free(pe, g, name)
                pe.wait_ge(p2_ready, 2 * g + q + 1)
                for t in range(4):
                    last = turn_over(ps(name)[:, P * t:P * t + P], e2[:, q, t, :], ident[:])
                last.then_inc(fulled(name), 1)

            def pool_tokens(g, q):
                pe.wait_ge(p1T_ready, 2 * g + q + 1)
                for k in range(2):
                    name = f"PX_{2 * q + k}"
                    wait_free(pe, g, name)
                    for t in range(2):
                        last = mm(ps(name)[:, 256 * t:256 * t + 256], xn[:, 4 * q + 2 * k + t, :],
                                  p1T[:, 2 * k + t, :, :], start=True, stop=True)
                    last.then_inc(fulled(name), 1)

            def scores(g, k):
                t, hh = k // 2, k % 2
                name = f"S_{k}"
                wait_free(pe, g, name)
                if k % T == 0:
                    pe.wait_ge(Qx_ready, 2 * g + 1 + k // T)
                mm(ps(name)[:], identb[:], maskb[:].rearrange("p h s -> p (h s)"), start=True, stop=False,
                   skip_group_check=True)
                for q in range(2):
                    for r in range(2):
                        b = 2 * t + r
                        last = mm(ps(name)[64 * r:64 * r + 64, 256 * q:256 * q + 256],
                                  Qx[:, 2 * hh + q, S * b:S * b + S], Kx[:, :, S * b:S * b + S],
                                  start=False, stop=True, skip_group_check=True)
                last.then_inc(fulled(name), 1)

            def turn(g, k):
                name = f"PT_{k}"
                wait_free(pe, g, name)
                pe.wait_ge(pn_ready, 2 * T * g + k + 1)
                src = pr[:, k % PR, :, :].rearrange("p h s -> p (h s)")
                for j in range(4):
                    last = turn_over(ps(name)[:, P * j:P * j + P], src[:, P * j:P * j + P], ident[:])
                last.then_inc(fulled(name), 1)

            def values(g, t):
                name = f"OL_{t}"
                wait_free(pe, g, name)
                for s in range(2):
                    pe.wait_ge(pT_ready, 2 * T * g + 2 * t + s + 1)
                    for gq in range(4):
                        j = 4 * s + gq
                        rr = slice(32 * gq, 32 * gq + 32)
                        p = pT[:, (2 * t + s) % 4, gq, :]
                        last = mm(ps(name)[rr, P * s:P * s + P], Vb[:, t, j, :, :].rearrange("p a c -> p (a c)"),
                                  p, start=True, stop=True, tile_position=(0, 32 * gq))
                last.then_inc(fulled(name), 1)

            def project(g, t):
                name = f"Yx_{t}"
                wait_free(pe, g, name)
                pe.wait_ge(On_ready, T * g + t + 1)
                for s in range(2):
                    for r in range(2):
                        last = mm(ps(name)[64 * r:64 * r + 64, 0:P], On[:, t % 2, s, 64 * r:64 * r + 64],
                                  woM[:, s, r, :], start=(s == 0), stop=(s == 1))
                last.then_inc(fulled(name), 1)

            def values_of(g, n):
                wait_free(pe, g, f"V_{n}")
                for k in range(4):
                    b = 4 * n + k
                    for r in range(2):
                        last = mm(ps(f"V_{n}")[64 * r:64 * r + 64, P * k:P * k + P],
                                  ctxT[:, S * b:S * b + S], xwT[:, 2, :], start=True, stop=True)
                last.then_inc(fulled(f"V_{n}"), 1)

            def keys_of(g, c):
                wait_free(pe, g, f"KT_{c}")
                mm(ps(f"KT_{c}")[:], xwT[:, 1, :], ctxT[:, 512 * c:512 * c + 512], start=True,
                   stop=True).then_inc(fulled(f"KT_{c}"), 1)

            def moments(g, n):
                A = A1 if n < 4 else A2
                wait_free_unless(g, f"M_{n}", "xnT1")
                for k in range(4):
                    last = mm(ps(f"M_{n}")[:, P * k:P * k + P], A[:, 4 * (n % 4) + k, :], pooled[:],
                              start=True, stop=True)
                last.then_inc(fulled(f"M_{n}"), 1)

            def both(e, g):
                if g is not None:
                    pe.wait_ge(c_loaded, 16 * g + 16)
                    four(g, "ctxT_0", cin, 0)
                    four(g, "ctxT_1", cin, 1)
                if e is not None:
                    turn(e, 2 * T - 2)
                    turn(e, 2 * T - 1)
                if g is not None:
                    pe.wait_ge(ctxT_ready, 2 * g + 2)
                    values_of(g, 0)
                if e is not None:
                    values(e, T - 1)
                if g is not None:
                    values_of(g, 1)
                if e is not None:
                    project(e, T - 1)
                if g is not None:
                    pe.wait_ge(xn_ready, 2 * g + 1)
                    four(g, "xnT1_0", xn, 0)
                    four(g, "xnT1_1", xn, 1)
                    values_of(g, 2)
                    values_of(g, 3)
                    keys_of(g, 0)
                    pe.wait_ge(pooled_ready, g + 1)
                    for n in range(4):
                        moments(g, n)
                if e is not None:
                    pe.wait_ge(xn3_ready, e + 1)
                    four(e, "xnT3_0", xn3, 0)
                    four(e, "xnT3_1", xn3, 1)
                if g is not None:
                    moments(g, 4)
                if e is not None:
                    pe.wait_ge(xnT3_ready, 2 * e + 2)
                    for t in range(T):
                        last = mm(ps("gate")[:, E * t:E * t + E], xnT3[:, P * t:P * t + P], gwT[:],
                                  start=True, stop=True)
                    last.then_inc(fulled("gate"), 1)
                if g is not None:
                    for n in (5, 6, 7):
                        moments(g, n)
                unit(e, 0)
                if g is not None:
                    scores_1(g, 0)
                    scores_1(g, 1)
                    scores_2(g, 0)
                    keys_of(g, 1)
                if e is not None:
                    up(e, 1)
                    down_to(e, 0)
                    wait_free(pe, e, "combS")
                    pe.wait_ge(comb_ready, e + 1)
                    for t in range(T):
                        last = turn_over(ps("combS")[:].bitcast(bf16)[:, P * t:P * t + P], combs[:, t, :], identb[:])
                    last.then_inc(fulled("combS"), 1)
                    pe.wait_ge(combT_ready, 3 * e + 1)
                    weight(e, 1)
                for k in (2, 3):
                    unit(e, k)
                if g is not None:
                    scores_1(g, 2)
                    scores_1(g, 3)
                    scores_2(g, 1)
                    unit(e, 4)
                    unit(e, 5)
                    turn_probs(g, 0)
                    unit(e, 6)
                    pool_tokens(g, 0)
                    turn_probs(g, 1)
                    unit(e, 7)
                    pool_tokens(g, 1)
                    unit(e, 8)
                    pe.wait_ge(PX_ready, 4 * g + 4)
                    for n in range(4):
                        wait_free_unless(g, f"UT_{n}", "PX")
                        for k in range(4):
                            h = 4 * n + k
                            last = mm(ps(f"UT_{n}")[:, P * k:P * k + P], Wvo[:, h, :],
                                      PX[:, :, POOL * h:POOL * h + POOL], start=True, stop=True)
                        last.then_inc(fulled(f"UT_{n}"), 1)
                    unit(e, 9)
                    pe.wait_ge(UT_ready, 4 * g + 4)
                    for n in range(4):
                        wait_free_unless(g, f"U_{n}", "UT")
                        for k in range(4):
                            last = turn_over(ps(f"U_{n}")[:, P * k:P * k + P], UT[:, 4 * n + k, :], ident[:])
                        last.then_inc(fulled(f"U_{n}"), 1)
                    unit(e, 10)
                    pe.wait_ge(p2T_ready, 2 * g + 2)
                    pe.wait_ge(U_ready, 4 * g + 4)
                    for q in range(Q):
                        wait_free_unless(g, f"Ya_{q}", "U")
                        for k in range(8):
                            b, r = 8 * q + k, k % 2
                            last = mm(ps(f"Ya_{q}")[64 * r:64 * r + 64, P * (k // 2):P * (k // 2) + P],
                                      p2T[:, S * b:S * b + S], U[:, b, :], start=True, stop=True)
                        last.then_inc(fulled(f"Ya_{q}"), 1)
                else:
                    for k in range(4, 11):
                        unit(e, k)
                for k in range(11, 16):
                    unit(e, k)
                if g is not None:
                    pe.wait_ge(xn_ready, 2 * g + 2)
                    four(g, "xnT2_0", xn, 0)
                    four(g, "xnT2_1", xn, 1)
                unit(e, 16)
                if g is not None:
                    for c in range(2):
                        wait_free(pe, g, f"QT_{c}")
                        pe.wait_ge(xnT_ready, 4 * g + 3 + c)
                        mm(ps(f"QT_{c}")[:], xwT[:, 0, :], xnT[:, 512 * c:512 * c + 512], start=True,
                           stop=True).then_inc(fulled(f"QT_{c}"), 1)
                unit(e, 17)
                if e is None:
                    pe.wait_ge(spread_wo, 16 * 16)
                    pe.wait_ge(loaded_m, 16 * 10)
                    pe.wait_ge(w_split, 4)
                if g is not None:
                    pe.wait_ge(Kx_ready, 2 * g + 2)
                    pe.wait_ge(V_ready, 4 * g + 4)
                    scores(g, 0)
                    scores(g, 1)
                if e is not None:
                    down_to(e, 17)
                if g is not None:
                    scores(g, 2)
                    scores(g, 3)
                    for t in range(T):
                        for k in (2 * t, 2 * t + 1):
                            if t:
                                turn(g, k - 2)
                            if t + 2 < T:
                                scores(g, k + 4)
                        if t:
                            values(g, t - 1)
                        if t >= 2:
                            project(g, t - 2)
                    project(g, T - 2)

            def wait_free_unless(g, name, waited):
                before = att[place[name][4] - 4]
                if not before.startswith(waited + "_"):
                    wait_free(pe, g, name)

            run(pe, both)

        @block.scalar
        def _(act):
            cp = nc.scalar.copy
            for n, w in enumerate((Wq, Wk, Wv, Wo_x)):
                act.dma_start(xw[:, n, :], w).then_inc(loaded_x, 16)
            act.dma_start(gw, gate_w).then_inc(loaded_x, 16)
            for n, (kind, s) in enumerate(SETUP):
                act.wait_ge(setup_ps, n + 1)
                src = two[n % 3][:].rearrange("p (k d) -> p k d", d=P)
                if kind == "T":
                    if s < 2:
                        diag = (diag_q, diag_k)[s]
                        if s == 0:
                            act.wait_ge(diag_cleared, 1)
                        for r in range(2):
                            rr = slice(64 * r, 64 * r + 64)
                            last = cp(diag[rr, :, P * r:P * r + P], src[rr])
                    if s != 1:
                        last = cp(wT[:, 8 * s:8 * s + 8, :], src)
                    last.then_inc(setup_cp, 1)
                elif kind == "W":
                    dst = (A1, A2, Wvo)[s // 2]
                    cp(dst[:, 8 * (s % 2):8 * (s % 2) + 8, :], src).then_inc(setup_cp, 1)
                else:
                    cp(xwT[:], src[:, 0:4, :])
                    cp(gwT[:], two[n % 3][:, 512:512 + E]).then_inc(setup_cp, 1)
            act.wait_ge(plane_ready, 1)

            def moved(g, name, dst, ready, src=None):
                wait_full(act, g, name)
                cp(dst, ps(name)[:] if src is None else src).then_inc(ready, 1)

            def silu(e, k):
                if e is None:
                    return
                wait_full(act, e, f"H1_{k}")
                nc.scalar.activation(sil[:, k % 2, :], ps(f"H1_{k}")[:], ACT.Silu,
                                     bias=b1[:, pair[k]:pair[k] + 1]).then_inc(sil_ready, 1)

            def probs_moved(g, q):
                wait_full(act, g, f"p1T_{q}")
                src = ps(f"p1T_{q}")[:].rearrange("p (t h) -> p t h", h=HI)
                cp(p1T[0:64, :, 0, :], src[0:64])
                cp(p1T[64:128, :, 1, :], src[64:128]).then_inc(p1T_ready, 1)
                moved(g, f"p2T_{q}", p2T[:, 512 * q:512 * q + 512], p2T_ready)

            def PX_moved(g, q):
                for n in (2 * q, 2 * q + 1):
                    moved(g, f"PX_{n}", PX[:, 4 * n:4 * n + 4, :], PX_ready,
                          ps(f"PX_{n}")[:].rearrange("p (b h) -> p b h", h=HI))

            def K_moved(g, n):
                if isinstance(g, int) and g == 0:
                    act.wait_ge(w_split, 4)
                wait_full(act, g, f"KT_{n}")
                for j in range(4):
                    last = nc.scalar.activation(Kx[:, j, 512 * n:512 * n + 512], ps(f"KT_{n}")[:], ACT.Copy,
                                                scale=plane[:, j:j + 1])
                last.then_inc(Kx_ready, 1)

            def V_moved(g, n):
                wait_full(act, g, f"V_{n}")
                src = ps(f"V_{n}")[:].rearrange("p (t a j r c) -> p t a j r c", t=2, a=2, r=2, c=XC)
                for r in range(2):
                    rr = slice(64 * r, 64 * r + 64)
                    for t in range(2):
                        last = cp(Vb[rr, 2 * n + t, :, :, XC * r:XC * r + XC],
                                  src[rr, t, :, :, r, :].rearrange("p a j c -> p j a c"))
                last.then_inc(V_ready, 1)

            def M_moved(g, n):
                h0 = POOL * 4 * (n % 4)
                moved(g, f"M_{n}", M[:, n // 4, :, h0:h0 + 4 * POOL].rearrange("p b (h i) -> p h b i", i=POOL),
                      M_ready, ps(f"M_{n}")[:].rearrange("p (h b i) -> p h b i", b=GB, i=POOL))

            def PT_moved(g, t):
                for k in (2 * t, 2 * t + 1):
                    moved(g, f"PT_{k}", pT[:, k % 4], pT_ready, ps(f"PT_{k}")[:].rearrange("p (j q) -> p j q", q=P))

            def O_moved(g, t):
                moved(g, f"OL_{t}", On[:, t % 2].rearrange("p s q -> p (s q)"), On_ready, ps(f"OL_{t}")[:, 0:2 * P])

            def Q_moved(g, n):
                wait_full(act, g, f"QT_{n}")
                for q in range(4):
                    rr = slice(32 * q, 32 * q + 32)
                    last = cp(Qx[rr, q, 512 * n:512 * n + 512], ps(f"QT_{n}")[rr, :])
                last.then_inc(Qx_ready, 1)

            def both(e, g):
                if g is not None:
                    for n in range(2):
                        moved(g, f"ctxT_{n}", ctxT[:, 512 * n:512 * n + 512], ctxT_ready)
                if e is not None:
                    PT_moved(e, T - 1)
                if g is not None:
                    V_moved(g, 0)
                if e is not None:
                    O_moved(e, T - 1)
                if g is not None:
                    V_moved(g, 1)
                    for n in range(2):
                        moved(g, f"xnT1_{n}", xnT[:, 512 * n:512 * n + 512], xnT_ready)
                    V_moved(g, 2)
                    V_moved(g, 3)
                    K_moved(g, 0)
                    for n in range(4):
                        M_moved(g, n)
                if e is not None:
                    for n in range(2):
                        moved(e, f"xnT3_{n}", xnT3[:, 512 * n:512 * n + 512], xnT3_ready)
                        cp(xnT3h[:, 512 * n:512 * n + 512], ps(f"xnT3_{n}")[:]).then_inc(hi_ready, 1)
                if g is not None:
                    M_moved(g, 4)
                if e is not None:
                    act.wait_ge(dg_ready, e + 1)
                    nc.scalar.activation(gex[:], ga[:], ACT.Exp).then_inc(gex_ready, 1)
                if g is not None:
                    for n in (5, 6, 7):
                        M_moved(g, n)
                silu(e, 0)
                if g is not None:
                    K_moved(g, 1)
                silu(e, 1)
                if e is not None:
                    moved(e, "combS", combsT[:], combT_ready, ps("combS")[:].bitcast(bf16))
                for k in range(2, 5):
                    silu(e, k)
                if g is not None:
                    for q in range(Q):
                        act.wait_ge(d1_ready, 4 * g + 2 * q + 2)
                        nc.scalar.activation(e1[:, q], e1[:, q], ACT.Exp, scale=AGENT_SCALE).then_inc(e1_ready, 1)
                        act.wait_ge(d2_ready, 2 * g + q + 1)
                        nc.scalar.activation(e2[:, q], e2[:, q], ACT.Exp, scale=AGENT_SCALE).then_inc(e2_ready, 1)
                silu(e, 5)
                if g is not None:
                    probs_moved(g, 0)
                silu(e, 6)
                if g is not None:
                    PX_moved(g, 0)
                    probs_moved(g, 1)
                silu(e, 7)
                if g is not None:
                    PX_moved(g, 1)
                silu(e, 8)
                if g is not None:
                    for n in range(4):
                        h0 = POOL * 4 * n
                        moved(g, f"UT_{n}", UT[:, :, h0:h0 + 4 * POOL].rearrange("p b (h i) -> p h b i", i=POOL),
                              UT_ready, ps(f"UT_{n}")[:].rearrange("p (h b i) -> p h b i", b=GB, i=POOL))
                silu(e, 9)
                if e is not None:
                    for n in range(2):
                        moved(e, f"combT_{n}", combT[0:2 * E, 512 * n:512 * n + 512], combT_ready,
                              ps(f"combT_{n}")[0:2 * E, :])
                for k in range(10, 16):
                    silu(e, k)
                if g is not None:
                    for n in range(2):
                        moved(g, f"xnT2_{n}", xnT[:, 512 * n:512 * n + 512], xnT_ready)
                silu(e, 16)
                if e is None:
                    act.wait_ge(consts, 4)
                    act.wait_ge(loaded_m, 16 * 10)
                if g is not None:
                    Q_moved(g, 0)
                silu(e, 17)
                if g is not None:
                    Q_moved(g, 1)
                    for t in range(T + 1):
                        if t < T:
                            act.wait_ge(mx_ready, T * g + t + 1)
                            for h in range(HALF):
                                last = nc.scalar.activation(pr[:, 2 * t % PR, h, :], ps(f"S_{2 * t}")[:, S * h:S * h + S],
                                                            ACT.Exp, bias=mx[:, 2 * t % 4, h:h + 1])
                            last.then_inc(pr_ready, 1)
                            act.wait_ge(dx_ready, T * g + t + 1)
                            p = pr[:, (2 * t + 1) % PR]
                            nc.scalar.activation(p, p, ACT.Exp).then_inc(pr_ready, 1)
                        if t >= 2:
                            O_moved(g, t - 2)
                        if 1 <= t < T:
                            PT_moved(g, t - 1)

            run(act, both)

        @block.vector
        def _(dve):
            V = nc.vector
            V.memset(PXUT[:], 0.0)
            V.memset(diag_o, 0.0).then_inc(diag_cleared, 1)
            dve.wait_ge(loaded_w, 16)
            dve.wait_ge(diag_cleared, 1)
            for r in range(2):
                rr = slice(64 * r, 64 * r + 64)
                V.tensor_copy(diag_o[rr, :, P * r:P * r + P], woa[rr]).then_inc(diag_ready, 1)
            dve.wait_ge(consts, 3)
            V.tensor_reduce(plane[:], planes[:], AX, ALU.add).then_inc(plane_ready, 1)
            links = {"a": 0, "e": 0}

            def link(ins, g, kind="a"):
                links[kind] += 1
                signal, per = (vec_a, LINKS_A) if kind == "a" else (vec_e, LINKS_E)
                ins.then_inc(signal, 1)
                dve.wait_ge(signal, per * g + links[kind])

            def norm(g, kind, src, var):
                mean, mean2, diff, diff2, sqd, sqd2, ve, _ = norms[kind]
                for t in range(T):
                    last = V.bn_stats(stats[kind][:, t, :], src[:, t, :])
                link(last, g, kind)
                even, odd = stats[kind][:, :, 0:3], stats[kind][:, :, 3:6]
                V.tensor_tensor(mean2[:], even[:, :, 1], odd[:, :, 1], ALU.add)
                V.tensor_tensor(diff[:], even[:, :, 1], odd[:, :, 1], ALU.subtract)
                link(V.tensor_tensor(sqd[:], even[:, :, 2], odd[:, :, 2], ALU.add), g, kind)
                V.tensor_scalar(mean[:], mean2[:], 0.5, None, ALU.mult)
                V.tensor_tensor(diff2[:], diff[:], diff[:], ALU.mult)
                link(V.tensor_scalar(sqd2[:], sqd[:], 1.0 / D, EPS, ALU.mult, ALU.add), g, kind)
                V.scalar_tensor_tensor(ve[:], diff2[:], 0.25, sqd2[:], ALU.mult, ALU.add).then_inc(var, 1)

            def apply(kind, src, dst, rstd_r, count, ready, halfway=lambda: None):
                mean, rstd = norms[kind][0], norms[kind][7]
                dve.wait_ge(rstd_r, count)
                for t in range(T):
                    if t == QT:
                        halfway()
                    last = V.tensor_scalar(dst[:, t, :], src[:, t, :], mean[:, t:t + 1], rstd[:, t:t + 1],
                                           ALU.subtract, ALU.mult)
                last.then_inc(ready, 1)

            def gate_shift(e):
                wait_full(dve, e, "gate")
                lg = ps("gate")[:, 0:T * E].rearrange("p (t e) -> p t e", e=E)
                link(V.tensor_reduce(g1[:], lg, AX, ALU.max), e, "e")
                V.tensor_tensor(ga[:], lg, g1[:].unsqueeze(2).to_broadcast([P, T, E]),
                                ALU.subtract).then_inc(dg_ready, 1)

            def gate(e):
                def link_e(ins):
                    link(ins, e, "e")

                te = [P, T, E]
                dve.wait_ge(gex_ready, e + 1)
                link_e(V.tensor_reduce(g3[:], gex[:], AX, ALU.add))
                link_e(V.reciprocal(g2[:], g3[:]))
                link_e(V.tensor_tensor(orig[:], gex[:], g2[:].unsqueeze(2).to_broadcast(te), ALU.mult))
                link_e(V.tensor_tensor(sc[:], orig[:], gb[:].unsqueeze(1).to_broadcast(te), ALU.add))
                sg = sc[:].rearrange("p t (g e) -> p (t g) e", e=EG)
                V.tensor_tensor(ps6[:, :, 0:2], sg[:, :, 0:2], sg[:, :, 2:4], ALU.add)
                V.tensor_tensor(ps6[:, :, 2:4], sg[:, :, 0:3:2], sg[:, :, 1:4:2], ALU.add)
                V.tensor_tensor(ps6[:, :, 4:5], sg[:, :, 0:1], sg[:, :, 3:4], ALU.add)
                link_e(V.tensor_tensor(ps6[:, :, 5:6], sg[:, :, 1:2], sg[:, :, 2:3], ALU.add))
                link_e(V.tensor_reduce(gs[:], ps6[:], AX, ALU.max))
                hidden(e, 0)
                gsv = gs[:].rearrange("p (t g) -> p t g", g=EG)
                for b in range(EG):
                    if b + 1 < EG:
                        V.tensor_tensor(beats[:, :, b + 1:, b], gsv[:, :, b:b + 1].to_broadcast([P, T, EG - 1 - b]),
                                        gsv[:, :, b + 1:], ALU.is_ge)
                    if b:
                        last = V.tensor_tensor(beats[:, :, 0:b, b], gsv[:, :, b:b + 1].to_broadcast([P, T, b]),
                                               gsv[:, :, 0:b], ALU.is_gt)
                link_e(last)
                link_e(V.tensor_reduce(rank[:], beats[:].rearrange("p t a b -> p (t a) b"), AX, ALU.add))
                link_e(V.tensor_scalar(kb[:], rank[:], 2.0, -FAR, ALU.is_ge, ALU.mult))
                link_e(V.tensor_tensor(tv[:].rearrange("p t (g e) -> p (t g) e", e=EG), sg,
                                       kb[:].unsqueeze(2).to_broadcast([P, T * EG, EG]), ALU.add))
                for k in range(2):
                    link_e(V.tensor_reduce(g1[:], tv[:], AX, ALU.max))
                    link_e(V.tensor_tensor(oh[:, k], tv[:], g1[:].unsqueeze(2).to_broadcast(te), ALU.is_equal))
                    link_e(V.tensor_tensor(oh[:, k], oh[:, k], down[:].unsqueeze(1).to_broadcast(te), ALU.mult))
                    link_e(V.tensor_reduce(g2[:], oh[:, k], AX, ALU.max))
                    link_e(V.tensor_tensor(oh[:, k], oh[:, k], g2[:].unsqueeze(2).to_broadcast(te), ALU.is_equal))
                    if k == 0:
                        link_e(V.scalar_tensor_tensor(tv[:], oh[:, 0], -FARTHER, tv[:], ALU.mult, ALU.add))
                link_e(V.tensor_tensor(tv[:], oh[:, 0], oh[:, 1], ALU.add))
                cw = comb[:, :, 0:E]
                part = [combs[:, :, E * k:E * k + E] for k in range(3)]
                V.tensor_tensor(cw, tv[:], orig[:], ALU.mult)
                link_e(V.tensor_tensor(part[0], tv[:], orig[:], ALU.mult))
                V.tensor_tensor(ga[:], cw, part[0], ALU.subtract)
                link_e(V.tensor_tensor(part[1], cw, part[0], ALU.subtract))
                V.tensor_tensor(part[2], ga[:], part[1], ALU.subtract).then_inc(comb_ready, 1)

            def hidden(e, k):
                if e is None:
                    return
                wait_full(dve, e, f"H3_{k}")
                dve.wait_ge(sil_ready, UNITS * e + k + 1)
                p = pair[k]
                if k not in PAIRED:
                    V.scalar_tensor_tensor(hT[:, k % 2, :], ps(f"H3_{k}")[:], b3[:, p:p + 1],
                                           sil[:, k % 2, :], ALU.add, ALU.mult).then_inc(hT_ready, 1)
                    return
                V.scalar_tensor_tensor(sil[:, k % 2, :], ps(f"H3_{k}")[:], b3[:, p:p + 1],
                                       sil[:, k % 2, :], ALU.add, ALU.mult).then_inc(hid_ready, 1)
                dve.wait_ge(hid_ready, len(PAIRED) * e + PAIRED.index(k) + 1)
                wait_full(dve, e, f"C_{k}")
                V.tensor_tensor(hT[:, k % 2, :], sil[:, k % 2, :], ps(f"C_{k}")[:], ALU.mult).then_inc(hT_ready, 1)

            def result(e, c):
                if e is None:
                    return
                wait_full(dve, e, f"Y_{c}")
                V.tensor_tensor(xo[:, 4 * c:4 * c + 4, :], xe[:, 4 * c:4 * c + 4, :],
                                ps(f"Y_{c}")[:].rearrange("p (t d) -> p t d", d=D), ALU.add).then_inc(out_ready, 1)

            def soften(g, q):
                for n in (2 * q, 2 * q + 1):
                    wait_full(dve, g, f"s1_{n}")
                    s1 = ps(f"s1_{n}")[:].rearrange("p (b s) -> p b s", s=P)[:, :, 0:S]
                    link(V.tensor_reduce(m1[:, n], s1, AX, ALU.max), g)
                    V.tensor_tensor(e1[:, q, 4 * (n % 2):4 * (n % 2) + 4], s1,
                                    m1[:, n].unsqueeze(2).to_broadcast([P, 4, S]), ALU.subtract).then_inc(d1_ready, 1)
                wait_full(dve, g, f"s2_{q}")
                s2 = ps(f"s2_{q}")[:].rearrange("p (k i) -> p k i", i=POOL)
                link(V.tensor_reduce(m2[:], s2, AX, ALU.max), g)
                V.tensor_tensor(e2[:, q].rearrange("p t (h i) -> p (t h) i", i=POOL), s2,
                                m2[:].unsqueeze(2).to_broadcast([P, QT * H, POOL]), ALU.subtract).then_inc(d2_ready, 1)

            def normalise_2(g, q):
                dve.wait_ge(e2_ready, 2 * g + q + 1)
                e2v = e2[:, q].rearrange("p t (h i) -> p (t h) i", i=POOL)
                link(V.tensor_reduce(l2[:], e2v, AX, ALU.add), g)
                link(V.reciprocal(r2[:], l2[:]), g)
                V.tensor_tensor(e2v, e2v, r2[:].unsqueeze(2).to_broadcast([P, QT * H, POOL]),
                                ALU.mult).then_inc(p2_ready, 1)

            def sums_1(g, q):
                dve.wait_ge(e1_ready, 2 * g + q + 1)
                link(V.tensor_reduce(l1[:], e1[:, q], AX, ALU.add), g)
                link(V.reciprocal(r1[:, 8 * q:8 * q + 8], l1[:]), g)

            def maxima(g, t):
                for k in (2 * t, 2 * t + 1):
                    wait_full(dve, g, f"S_{k}")
                    sv = ps(f"S_{k}")[:].rearrange("p (h s) -> p h s", s=S)
                    if k % 2 == 0:
                        V.tensor_reduce(mx[:, k % 4], sv, AX, ALU.max, negate=True).then_inc(mx_ready, 1)
                    else:
                        link(V.tensor_reduce(mx[:, k % 4], sv, AX, ALU.max), g)
                        V.tensor_tensor(pr[:, k % PR], sv, mx[:, k % 4].unsqueeze(2).to_broadcast([P, HALF, S]),
                                        ALU.subtract).then_inc(dx_ready, 1)

            def inverses(g, t):
                for k in (2 * t, 2 * t + 1):
                    dve.wait_ge(pr_ready, 2 * T * g + k + 1)
                    link(V.tensor_reduce(lx[:, k % 4], pr[:, k % PR], AX, ALU.add), g)
                    V.reciprocal(rx[:, k % 4], lx[:, k % 4]).then_inc(rx_ready, 1)

            def add_x(g, t):
                wait_full(dve, g, f"Yx_{t}")
                V.tensor_tensor(xe[:, t, :], xr[:, t, :], ps(f"Yx_{t}")[:, 0:P], ALU.add).then_inc(xattn_added, 1)

            def both(e, g):
                links["a"] = links["e"] = 0
                if e is not None:
                    add_x(e, T - 3)
                if g is not None:
                    dve.wait_ge(x_loaded, 16 * g + 16)
                    norm(g, "a", xin, var_ready)
                if e is not None:
                    add_x(e, T - 2)
                if g is not None:
                    apply("a", xin, xn, rstd_ready, 2 * g + 1, xn_ready)
                if e is None:
                    dve.wait_ge(loaded_m, 16 * 10)
                    dve.wait_ge(loaded_e, 16 * 4)
                    for n, (w, wh, wl) in enumerate(((w1, w1h, w1l), (w3, w3h, w3l))):
                        V.tensor_copy(wh[:], w).then_inc(w_split, 1)
                        dve.wait_ge(w_split, 2 * n + 1)
                        V.tensor_tensor(wl[:], w, wh[:].bitcast(fp32), ALU.subtract).then_inc(w_split, 1)
                if e is not None:
                    add_x(e, T - 1)
                    dve.wait_ge(xattn_added, T * e + T)
                    norm(e, "e", xe, var3_ready)
                if g is not None:
                    dve.wait_ge(xnT_ready, 4 * g + 2)
                    V.tensor_reduce(pooled[:], xnT[:, 0:TOK].rearrange("p (k s) -> p k s", s=S // POOL), AX,
                                    ALU.add).then_inc(pooled_ready, 1)
                if e is not None:
                    apply("e", xe, xn3, rstd3_ready, e + 1, xn3_ready)
                    gate_shift(e)
                    gate(e)
                if g is not None:
                    soften(g, 0)
                for k in range(1, 4):
                    hidden(e, k)
                if g is not None:
                    soften(g, 1)
                    hidden(e, 4)
                    normalise_2(g, 0)
                    hidden(e, 5)
                    normalise_2(g, 1)
                    hidden(e, 6)
                    for q in range(Q):
                        sums_1(g, q)
                    for k in (7, 8, 9):
                        hidden(e, k)
                    result(e, 0)
                    for n in range(4):
                        wait_full(dve, g, f"U_{n}")
                        V.tensor_tensor(U[:, 4 * n:4 * n + 4, :], ps(f"U_{n}")[:].rearrange("p (b d) -> p b d", d=D),
                                        r1[:, 4 * n:4 * n + 4].unsqueeze(2).to_broadcast([P, 4, D]),
                                        ALU.mult).then_inc(U_ready, 1)
                    hidden(e, 10)
                    dve.wait_ge(xr_ready, g + 1)
                    for q in range(Q):
                        wait_full(dve, g, f"Ya_{q}")
                        V.tensor_tensor(xr[:, 4 * q:4 * q + 4, :], xr[:, 4 * q:4 * q + 4, :],
                                        ps(f"Ya_{q}")[:].rearrange("p (t d) -> p t d", d=D),
                                        ALU.add).then_inc(attn_added, 1)
                    dve.wait_ge(attn_added, 2 * g + 2)
                    hidden(e, 11)
                    norm(g, "a", xr, var_ready)
                    hidden(e, 12)
                    apply("a", xr, xn, rstd_ready, 2 * g + 2, xn_ready, lambda: hidden(e, 13))
                else:
                    for k in range(4, 10):
                        hidden(e, k)
                    result(e, 0)
                    for k in range(10, 14):
                        hidden(e, k)
                for k in range(14, 18):
                    hidden(e, k)
                if g is None:
                    result(e, 1)
                if g is not None:
                    for t in range(T + 1):
                        if t >= 4:
                            add_x(g, t - 4)
                        if t < T:
                            maxima(g, t)
                        if t == 0:
                            result(e, 1)
                        if t:
                            inverses(g, t - 1)
                    assert links["a"] == LINKS_A, links
                if e is not None:
                    dve.wait_ge(stored, 16 * CHUNKS * (e + 1))
                    assert links["e"] == LINKS_E, links

            run(dve, both)


_INS = ['x', 'ctx_1024', 'L0_attn_Wqkv', 'L0_attn_Wo', 'L0_attn_bo', 'L0_xattn_Wq', 'L0_xattn_Wk', 'L0_xattn_Wv',
        'L0_xattn_Wo', 'L0_ffn_gate_w', 'L0_ffn_gate_b', 'L0_ffn_We1', 'L0_ffn_be1', 'L0_ffn_We2', 'L0_ffn_be2',
        'L0_ffn_We3', 'L0_ffn_be3', 'L0_ffn_ws1', 'L0_ffn_bs1', 'L0_ffn_ws2', 'L0_ffn_bs2', 'L0_ffn_ws3', 'L0_ffn_bs3']


def kernel(**inputs):
    import concourse.bacc as bacc
    from concourse.bass_utils import run_bass_kernel_spmd

    nc = bacc.Bacc("TRN2", target_bir_lowering=False, num_devices=1)
    arrays, args = {}, []
    for name in _INS:
        a = np.ascontiguousarray(inputs[name])
        arrays[f"in_{name}"] = a
        args.append(nc.dram_tensor(f"in_{name}", a.shape, mybir.dt.from_np(a.dtype), kind="ExternalInput").ap())
    out = nc.dram_tensor("out_x", arrays["in_x"].shape, mybir.dt.float32, kind="ExternalOutput").ap()
    decoder_block(nc, *args, out)
    r = run_bass_kernel_spmd(nc, [arrays], core_ids=[0])
    return r.results[0]["out_x"]
```
